# Optimizing a Trainium2 kernel written in Bass

```python
import numpy as np
import jax
import jax.numpy as jnp

def _softmax(x, axis=-1):
    return jax.nn.softmax(x, axis=axis)

def _gelu(x):
    return jax.nn.gelu(x, approximate=True)

def _silu(x):
    return jax.nn.silu(x)

def _sigmoid(x):
    return jax.nn.sigmoid(x)

def _layernorm(x, axis=-1, eps=1e-05):
    m = jnp.mean(x, axis=axis, keepdims=True)
    v = jnp.var(x, axis=axis, keepdims=True)
    return (x - m) / jnp.sqrt(v + eps)

def _scatter_add(tgt, idx, src, axis=0):
    return tgt.at[idx].add(src)

def _segment_sum(src, seg, n):
    return jax.ops.segment_sum(src, seg, n)
kernel_name = 'mk_vit_tower_postln_d1_tok_img768_r4_76e0e3'

def setup_inputs(seed: int=0):
    np.random.seed(seed)
    _w = jnp.asarray

    def _rec_inputs():
        import jax
        import jax.numpy as jnp
        _rk = jax.random.key(seed)
        x = -9.25966e-05 + 0.999892 * jax.random.normal(jax.random.fold_in(_rk, 1), (64, 3, 112, 112), jnp.float32)
        return x
    x = _rec_inputs()

    def _L0_tok_setup():
        import jax, jax.numpy as jnp
        import numpy as np
        PATCH = 16
        EMBED = 192
        key = jax.random.key(seed)
        k1, k2 = jax.random.split(key)
        x = jax.random.normal(k1, (64, 3, 128, 96), dtype=jnp.float32)
        W = jax.random.normal(k2, (EMBED, 3 * PATCH * PATCH), dtype=jnp.float32) * (1.0 / np.sqrt(3 * PATCH * PATCH))
        return {'x': x, 'W': W}
    _L0_tok_all = _L0_tok_setup()
    _L0_tok_in = {k: v for k, v in _L0_tok_all.items() if k in ('W',)}
    del _L0_tok_all

    def _L0_attn_setup():
        import jax, jax.numpy as jnp
        import numpy as np
        N_HEAD = 12
        key = jax.random.key(seed)
        ks = jax.random.split(key, 6)
        B, T, C = (8, 256, 192)
        x = jax.random.normal(ks[0], (B, T, C), dtype=jnp.float32)
        w_attn = jax.random.normal(ks[1], (C, 3 * C), dtype=jnp.float32) * 0.02
        b_attn = jnp.zeros((3 * C,), dtype=jnp.float32)
        w_proj = jax.random.normal(ks[2], (C, C), dtype=jnp.float32) * 0.02
        b_proj = jnp.zeros((C,), dtype=jnp.float32)
        rel_emb = jax.random.normal(ks[3], (2 * 256 - 1, C // N_HEAD), dtype=jnp.float32) * 0.02
        return {'x': x, 'w_attn': w_attn, 'b_attn': b_attn, 'w_proj': w_proj, 'b_proj': b_proj, 'rel_emb': rel_emb}
    _L0_attn_all = _L0_attn_setup()
    _L0_attn_in = {k: v for k, v in _L0_attn_all.items() if k in ('w_attn', 'b_attn', 'w_proj', 'b_proj', 'rel_emb')}
    del _L0_attn_all

    def _L0_ffn_setup():
        import jax, jax.numpy as jnp
        import numpy as np
        DIM = 192
        NUM_HEADS = 12
        HEAD_DIM = DIM // NUM_HEADS
        SCALE = HEAD_DIM ** (-0.5)
        NUM_EXPERTS = 8
        RANK = 16
        ALPHA = 32
        TOPK = 2
        SCALING = ALPHA / RANK
        B, S = (8, 256)
        key = jax.random.key(seed)
        ks = jax.random.split(key, 12)
        d, e, r = (DIM, NUM_EXPERTS, RANK)
        inp = {'x': jax.random.normal(ks[0], (B, S, d), jnp.float32), 'Wg': jax.random.normal(ks[1], (e, d), jnp.float32) * 0.02, 'bg': jax.random.normal(ks[2], (e,), jnp.float32) * 0.02, 'Wqkv': jax.random.normal(ks[3], (3 * d, d), jnp.float32) * 0.02, 'bqkv': jax.random.normal(ks[4], (3 * d,), jnp.float32) * 0.02, 'Wproj': jax.random.normal(ks[5], (d, d), jnp.float32) * 0.02, 'bproj': jax.random.normal(ks[6], (d,), jnp.float32) * 0.02, 'A': jax.random.normal(ks[7], (e, r, d), jnp.float32) * 0.05, 'ba': jax.random.normal(ks[8], (e, r), jnp.float32) * 0.02, 'Bm': jax.random.normal(ks[9], (e, 3 * d, r), jnp.float32) * 0.05, 'bb': jax.random.normal(ks[10], (e, 3 * d), jnp.float32) * 0.02}
        return inp
    _L0_ffn_all = _L0_ffn_setup()
    _L0_ffn_in = {k: v for k, v in _L0_ffn_all.items() if k in ('Wg', 'bg', 'Wqkv', 'bqkv', 'Wproj', 'bproj', 'A', 'ba', 'Bm', 'bb')}
    del _L0_ffn_all
    return {'x': x, 'L0_tok_W': _L0_tok_in['W'], 'L0_attn_w_attn': _L0_attn_in['w_attn'], 'L0_attn_b_attn': _L0_attn_in['b_attn'], 'L0_attn_w_proj': _L0_attn_in['w_proj'], 'L0_attn_b_proj': _L0_attn_in['b_proj'], 'L0_attn_rel_emb': _L0_attn_in['rel_emb'], 'L0_ffn_Wg': _L0_ffn_in['Wg'], 'L0_ffn_bg': _L0_ffn_in['bg'], 'L0_ffn_Wqkv': _L0_ffn_in['Wqkv'], 'L0_ffn_bqkv': _L0_ffn_in['bqkv'], 'L0_ffn_Wproj': _L0_ffn_in['Wproj'], 'L0_ffn_bproj': _L0_ffn_in['bproj'], 'L0_ffn_A': _L0_ffn_in['A'], 'L0_ffn_ba': _L0_ffn_in['ba'], 'L0_ffn_Bm': _L0_ffn_in['Bm'], 'L0_ffn_bb': _L0_ffn_in['bb']}

def reference(x, L0_tok_W, L0_attn_w_attn, L0_attn_b_attn, L0_attn_w_proj, L0_attn_b_proj, L0_attn_rel_emb, L0_ffn_Wg, L0_ffn_bg, L0_ffn_Wqkv, L0_ffn_bqkv, L0_ffn_Wproj, L0_ffn_bproj, L0_ffn_A, L0_ffn_ba, L0_ffn_Bm, L0_ffn_bb):
    import jax
    import jax.numpy as jnp

    def _L0_tok_ref(x, W):
        import jax, jax.numpy as jnp
        import numpy as np
        PATCH = 16
        EMBED = 192
        B, C, H, Wd = x.shape
        p = PATCH
        hp, wp = (H // p, Wd // p)
        patches = x.reshape(B, C, hp, p, wp, p).transpose(0, 1, 2, 4, 3, 5)
        patches = patches.reshape(B, C, hp * wp, p, p).transpose(0, 2, 1, 3, 4)
        patches = patches.reshape(B, hp * wp, C * p * p)
        return jnp.einsum('bnd,ed->bne', patches, W)

    def _L0_attn_ref(x, w_attn, b_attn, w_proj, b_proj, rel_emb):
        import jax, jax.numpy as jnp
        import numpy as np
        N_HEAD = 12
        b, t, c = x.shape
        h = N_HEAD
        d = c // h
        scale = d ** (-0.5)
        qkv = x @ w_attn + b_attn
        q, k, v = jnp.split(qkv, 3, axis=-1)
        split_heads = lambda z: z.reshape(b, t, h, d).transpose(0, 2, 1, 3)
        q, k, v = map(split_heads, (q, k, v))
        q = q * scale
        scores = jnp.einsum('bhid,bhjd->bhij', q, k)
        rel = rel_emb[:t]
        rel = jnp.concatenate([jnp.zeros_like(rel[:1]), rel], axis=0)[:-1]
        scores = scores + jnp.einsum('bhid,jd->bhij', q, rel)
        causal = jnp.tril(jnp.ones((t, t), dtype=bool))
        scores = jnp.where(causal, scores, -jnp.inf)
        probs = jax.nn.softmax(scores, axis=-1)
        y = jnp.einsum('bhij,bhjd->bhid', probs, v)
        y = y.transpose(0, 2, 1, 3).reshape(b, t, c)
        return y @ w_proj + b_proj

    def _L0_ffn_ref(x, Wg, bg, Wqkv, bqkv, Wproj, bproj, A, ba, Bm, bb):
        import jax, jax.numpy as jnp
        import numpy as np
        DIM = 192
        NUM_HEADS = 12
        HEAD_DIM = DIM // NUM_HEADS
        SCALE = HEAD_DIM ** (-0.5)
        NUM_EXPERTS = 8
        RANK = 16
        ALPHA = 32
        TOPK = 2
        SCALING = ALPHA / RANK
        B, S = (8, 256)
        b, s, d = x.shape
        t = b * s
        xf = x.reshape(t, d)
        probs = jax.nn.softmax(xf @ Wg.T + bg, axis=-1)
        top_w, top_idx = jax.lax.top_k(probs, TOPK)
        combine = jnp.zeros((t, NUM_EXPERTS), x.dtype).at[jnp.arange(t)[:, None], top_idx].add(top_w)
        h = jnp.einsum('td,erd->ter', xf, A) + ba
        hw = h * combine[:, :, None]
        delta = jnp.einsum('ter,eor->to', hw, Bm) + combine @ bb
        delta = delta * SCALING
        qkv = xf @ Wqkv.T + bqkv + delta
        qkv = qkv.reshape(b, s, 3, NUM_HEADS, HEAD_DIM)
        qkv = jnp.transpose(qkv, (2, 0, 3, 1, 4))
        q, k, v = (qkv[0], qkv[1], qkv[2])
        attn = jax.nn.softmax(jnp.einsum('bhsd,bhtd->bhst', q, k) * SCALE, axis=-1)
        out = jnp.einsum('bhst,bhtd->bhsd', attn, v)
        out = jnp.transpose(out, (0, 2, 1, 3)).reshape(b, s, d)
        return out @ Wproj.T + bproj
    h = _L0_tok_ref(x, L0_tok_W)
    h = _layernorm(h + _L0_attn_ref(h, L0_attn_w_attn, L0_attn_b_attn, L0_attn_w_proj, L0_attn_b_proj, L0_attn_rel_emb), axis=-1)
    h = _layernorm(h + _L0_ffn_ref(h, L0_ffn_Wg, L0_ffn_bg, L0_ffn_Wqkv, L0_ffn_bqkv, L0_ffn_Wproj, L0_ffn_bproj, L0_ffn_A, L0_ffn_ba, L0_ffn_Bm, L0_ffn_bb), axis=-1)
    return h

_drawn_inputs = setup_inputs


def setup_inputs(seed=0):
    import zlib

    import numpy as np

    out = dict(_drawn_inputs(seed))
    spreads = {'L0_attn_b_attn': (0.0, 0.267), 'L0_attn_b_proj': (0.0, 0.1)}
    factors = {'L0_attn_rel_emb': 8.0,
     'L0_ffn_Wg': 8.0,
     'L0_ffn_bg': 8.0,
     'L0_ffn_Wqkv': 3.971,
     'L0_ffn_bqkv': 8.0,
     'L0_ffn_Wproj': 3.498,
     'L0_ffn_bproj': 21.832,
     'L0_ffn_A': 8.0,
     'L0_ffn_ba': 8.0,
     'L0_ffn_Bm': 8.0,
     'L0_ffn_bb': 8.0}
    for name, (base, spread) in spreads.items():
        noise = np.random.default_rng([zlib.crc32(name.encode()), seed]).standard_normal(out[name].shape)
        drawn = base * np.exp(spread * noise) if base else spread * noise
        out[name] = jnp.asarray(drawn.astype(out[name].dtype))
    for name, factor in factors.items():
        out[name] = (out[name] * factor).astype(out[name].dtype)
    return out
```

```python
from contextlib import ExitStack

import concourse.bass as bass
from concourse import mybir

F32 = mybir.dt.float32
BF16 = mybir.dt.bfloat16
U32 = mybir.dt.uint32
ALU = mybir.AluOpType
ACT = mybir.ActivationFunctionType
AX = mybir.AxisListType


def build(nc, x, tok_w, w_attn, b_attn, w_proj, b_proj, rel_emb, wg, bg, wqkv, bqkv, wproj2, bproj2,
          lora_a, lora_ba, lora_b, lora_bb, out):
    NB, CH, HI, WI = x.shape
    E, PD = tok_w.shape
    PATCH = 16
    HP, WP = HI // PATCH, WI // PATCH
    S = HP * WP
    SEQ = 2
    T = SEQ * S
    TILES = NB // SEQ
    GB = 16
    GROUPS = NB // GB
    GT = GB // SEQ
    GP = HP * GB
    H = 12
    D = E // H
    C = E // 2
    HC = H // 2
    KX = PD // 128
    NE, R, _ = lora_a.shape
    ER = NE * R
    QKV = 3 * E
    PB = 64
    PP = PB + S
    PAIRS = H // 2
    SCALE = float(D) ** -0.5
    LORA_SCALE = 32 / R
    EPS = 1e-5
    NEG = -1e30
    assert PD == KX * 128 and S <= PB and D * 2 == 32 and ER == 128 and 6 * 98 == H * S

    with ExitStack() as ctx:
        def sb(name, shape, dt=F32):
            return ctx.enter_context(nc.sbuf_tensor(name, shape, dt))

        def sem(name):
            return ctx.enter_context(nc.semaphore(name))

        ps = ctx.enter_context(nc.psum_tensor("ps", [128, 8, 512], F32))

        ident = sb("ident", [128, 128])
        ident_bf = sb("ident_bf", [128, 128], BF16)
        causal = sb("causal", [128, HC * S], BF16)
        headmask = sb("headmask", [C, HC])
        iota8i = sb("iota8i", [PP, NE], mybir.dt.int32)
        iota8 = sb("iota8", [PP, NE])
        eps_col = sb("eps_col", [T, 1])
        two_rows = sb("two_rows", [1 + NE, 1])

        tokw_raw = sb("tokw_raw", [C, 2, PD])
        xr = sb("xr", [GP, CH * WP, PATCH * PATCH])
        xr_flat = xr[0:C].rearrange("p a b -> p (a b)")
        wqkv_raw = xr_flat[:, 0:6 * E].rearrange("p (m k) -> p m k", m=6)
        wproj_raw = xr_flat[:, 6 * E:8 * E].rearrange("p (m k) -> p m k", m=2)
        bm_raw = xr_flat[:, 8 * E:8 * E + 6 * ER].rearrange("p (m e r) -> p m e r", m=6, e=NE)
        a_raw = sb("a_raw", [ER, E])
        g_raw = sb("g_raw", [NE, E])
        b6_raw = sb("b6_raw", [6, C])
        rel_raw = sb("rel_raw", [S, HC, D])
        ext_raw = sb("ext_raw", [1 + NE, QKV])
        tokw = sb("tokw", [128, KX, E])
        w1 = sb("w1", [C, 2, QKV])
        p1 = sb("p1", [C + 1, 2, E])
        b6 = sb("b6", [C, 6])
        qbias = sb("qbias", [C, 2])
        relt = sb("relt", [C, S])
        relk = sb("relk", [C, 2, S])
        w2 = sb("w2", [C + 1 + NE, 2, QKV])
        b2 = sb("b2", [ER, QKV])
        p2 = sb("p2", [C + 1, 2, E])
        lora = sb("lora", [C + 1, 2, ER + NE])

        xb = [sb(f"xb{u}", [GP, CH, PATCH * WI]) for u in range(2)]
        xt = sb("xt", [128, KX, GB * S])
        hstage = [sb(f"hstage{u}", [T, E]) for u in range(2)]
        h_all = sb("h_all", [T, TILES * E])
        ht_all = sb("ht_all", [C, TILES * 2 * T])

        class Layer:

            def __init__(self, n, bank):
                self.bq, self.bm, self.bs = bank, bank + 1, bank + 2
                self.ht = sb(f"ht{n}", [C + 1 + NE, 2, 128])
                self.qt = sb(f"qt{n}", [C, 2, T])
                self.kt = sb(f"kt{n}", [C, 2, T])
                self.kbd = sb(f"kbd{n}", [C, 2, SEQ, HC, S])
                self.vbd = sb(f"vbd{n}", [128, SEQ, E])
                self.mx = sb(f"mx{n}", [PP, H])
                self.p = sb(f"probs{n}", [PP, H, 64])
                self.sum = sb(f"sum{n}", [PP, H])
                self.rsum = sb(f"rsum{n}", [PP, H])
                self.pt = sb(f"pt{n}", [PP, PAIRS, PP])
                self.yt = sb(f"yt{n}", [C + 1, 2, T])
                self.res = sb(f"res{n}", [T, E])
                self.st = sb(f"st{n}", [T, 6])
                self.pad = sb(f"pad{n}", [1, 1])
                self.mv = sb(f"mv{n}", [T, 2])
                self.lnv = sb(f"lnv{n}", [T, 1])
                self.rstd = sb(f"rstd{n}", [T, 1])
                self.ht_ready = sem(f"ht_ready{n}")
                self.qk_done = sem(f"qk_done{n}")
                self.v_done = sem(f"v_done{n}")
                self.q_ready = sem(f"q_ready{n}")
                self.k_ready = sem(f"k_ready{n}")
                self.kbd_ready = sem(f"kbd_ready{n}")
                self.v_ready = sem(f"v_ready{n}")
                self.scores_done = sem(f"scores_done{n}")
                self.mx_ready = sem(f"mx_ready{n}")
                self.sub_ready = sem(f"sub_ready{n}")
                self.exp_ready = sem(f"exp_ready{n}")
                self.sum_ready = sem(f"sum_ready{n}")
                self.rsum_ready = sem(f"rsum_ready{n}")
                self.p_ready = sem(f"p_ready{n}")
                self.ptr_done = sem(f"ptr_done{n}")
                self.pt_ready_a = sem(f"pt_ready_a{n}")
                self.pt_ready_b = sem(f"pt_ready_b{n}")
                self.pv_done = sem(f"pv_done{n}")
                self.yt_ready = sem(f"yt_ready{n}")
                self.proj_done = sem(f"proj_done{n}")
                self.res_ready = sem(f"res_ready{n}")
                self.st_ready = sem(f"st_ready{n}")
                self.mv_ready = sem(f"mv_ready{n}")
                self.lnv_ready = sem(f"lnv_ready{n}")
                self.rstd_ready = sem(f"rstd_ready{n}")
                self.ln_ready = sem(f"ln_ready{n}")

        L1 = Layer(1, 0)
        L2 = Layer(2, 4)
        h1s = sb("h1s", [T, E])
        o_sb = sb("o_sb", [T, E])
        hwt = sb("hwt", [ER, 128])
        nmax = sb("nmax", [PP, 1])
        ex = sb("ex", [PP, NE])
        esum = sb("esum", [PP, 1])
        resum = sb("resum", [PP, 1])
        top8 = sb("top8", [PP, 8])
        idx8 = sb("idx8", [PP, 8], U32)
        idxf = sb("idxf", [PP, 2])
        en = sb("en", [PP, NE])
        pick0 = sb("pick0", [PP, NE])
        pick1 = sb("pick1", [PP, NE])
        comb = sb("comb", [PP, 1 + NE])
        hw = sb("hw", [PP, ER])

        tokw_loaded = sem("tokw_loaded")
        weights_loaded = sem("weights_loaded")
        x_loaded = [sem(f"x_loaded{u}") for u in range(2)]
        rel_zeroed = sem("rel_zeroed")
        pool_step = sem("pool_step")
        consts_ready = sem("consts_ready")
        dve_consts = sem("dve_consts")
        prep_tr = sem("prep_tr")
        prep_act = sem("prep_act")
        prep_dve = sem("prep_dve")
        prep_extra = sem("prep_extra")
        xr_ready = sem("xr_ready")
        xtr_done = sem("xtr_done")
        xt_act = sem("xt_act")
        xt_dve = sem("xt_dve")
        emb_done = sem("emb_done")
        hstage_ready = sem("hstage_ready")
        htr_done = sem("htr_done")
        htall_ready = sem("htall_ready")
        hall_ready = sem("hall_ready")
        tr2_done = sem("tr2_done")
        lora_done = sem("lora_done")
        nmax_ready = sem("nmax_ready")
        ex_ready = sem("ex_ready")
        router_step = sem("router_step")
        hw_ready = sem("hw_ready")
        hwtr_done = sem("hwtr_done")
        hwt_ready = sem("hwt_ready")
        h1_kept = sem("h1_kept")
        out_stored = sem("out_stored")

        W_DMAS = 27

        prep = []
        for half in range(2):
            for k in range(0, KX, 3):
                prep.append(([(tokw_raw[:, half, (k + j) * 128:(k + j + 1) * 128], j * C) for j in range(3)],
                             128, 3 * C, tokw[:, k:k + 3, half * C:(half + 1) * C], 1.0))
        TOK_PREP = len(prep)
        for kc in range(2):
            for m in range(0, 6, 3):
                prep.append(([(wqkv_raw[:, m + j, kc * C:(kc + 1) * C], j * C) for j in range(3)],
                             C, 3 * C, w2[0:C, kc, m * C:(m + 3) * C], 1.0))
        for m in range(0, 6, 3):
            prep.append(([(bm_raw[:, m + j, :, :].rearrange("p e r -> p (e r)"), j * C) for j in range(3)],
                         ER, 3 * C, b2[:, m * C:(m + 3) * C], LORA_SCALE))
        for kc in range(2):
            prep.append(([(wproj_raw[:, j, kc * C:(kc + 1) * C], j * C) for j in range(2)],
                         C, 2 * C, p2[0:C, kc, :], 1.0))
            prep.append(([(a_raw[:, kc * C:(kc + 1) * C], 0), (g_raw[:, kc * C:(kc + 1) * C], ER)],
                         C, ER + NE, lora[0:C, kc, :], 1.0))
        prep.append(([(b6_raw[:, :], 0)], C, 6, b6[:, :], 1.0))
        prep.append(([(rel_raw[:, :, :].rearrange("p h d -> p (h d)"), 0)], C, S, relt[:, :], 1.0))
        N_PREP = len(prep)
        XE = 2 * WP

        def run(eng, iteration):
            for i in range(4):
                iteration(i, lambda s, i=i: i >= s)
            with eng.Fori(4, TILES) as i:
                iteration(i, lambda s: True)
            for i in range(TILES, TILES + 3):
                iteration(i, lambda s, i=i: i - s < TILES)

        def at(eng, semaphore, n):
            if not (isinstance(n, int) and n <= 0):
                eng.wait_ge(semaphore, n)

        block = ctx.enter_context(nc.Block())

        @block.sync
        def _(sp):
            def load_x(g):
                src = x[g * GB:(g + 1) * GB].rearrange("b c (h q) w -> h b c (q w)", q=PATCH)
                for hp in range(HP):
                    sp.dma_start(xb[g % 2][hp * GB:(hp + 1) * GB], src[hp]).then_inc(x_loaded[g % 2], 16)

            sp.dma_start(tokw_raw[:], tok_w.rearrange("(h p) k -> p h k", p=C)).then_inc(tokw_loaded, 16)
            load_x(0)

            def load_w(dst, src):
                sp.dma_start(dst, src).then_inc(weights_loaded, 16)

            load_w(w1[:], w_attn.rearrange("(k p) n -> p k n", p=C))
            load_w(p1[0:C], w_proj.rearrange("(k p) n -> p k n", p=C))
            load_w(p1[C:C + 1, 0, :], b_proj.unsqueeze(0))
            load_w(b6_raw[:], b_attn.rearrange("(m p) -> m p", p=C))
            sp.wait_ge(rel_zeroed, 1)
            for h in range(HC):
                load_w(rel_raw[1:S, h, :], rel_emb[0:S - 1])
            load_w(wqkv_raw, wqkv.rearrange("(m p) k -> p m k", p=C))
            load_w(ext_raw[0:1], bqkv.unsqueeze(0))
            load_w(ext_raw[1:1 + NE], lora_bb)
            load_w(wproj_raw, wproj2.rearrange("(m p) k -> p m k", p=C))
            load_w(p2[C:C + 1, 0, :], bproj2.unsqueeze(0))
            load_w(a_raw[:], lora_a.rearrange("e r k -> (e r) k"))
            load_w(g_raw[:], wg)
            load_w(lora[C:C + 1, 0, 0:ER], lora_ba.rearrange("e r -> (e r)").unsqueeze(0))
            load_w(lora[C:C + 1, 0, ER:ER + NE], bg.unsqueeze(0))
            for e in range(NE):
                load_w(bm_raw[:, :, e, :], lora_b[e].rearrange("(m p) r -> p m r", p=C))
            load_x(1)
            for g in range(2, GROUPS):
                sp.wait_ge(xr_ready, CH * (g - 1))
                load_x(g)

            out_rows = out.rearrange("b n e -> (b n) e")
            with sp.Fori(0, TILES) as t:
                sp.wait_ge(L2.ln_ready, t + 1)
                sp.dma_start(out_rows[bass.ds(t * T, T)], o_sb[:]).then_inc(out_stored, 16)
            sp.wait_ge(out_stored, 16 * TILES)

        @block.gpsimd
        def _(pool):
            steps = [0]

            def step(ins):
                steps[0] += 1
                ins.then_inc(pool_step, 1)
                pool.wait_ge(pool_step, steps[0])

            nc.gpsimd.memset(rel_raw[:], 0.0).then_inc(rel_zeroed, 1)
            step(nc.gpsimd.memset(ident[:], 0.0))
            step(nc.gpsimd.affine_select(out=ident[:], in_=ident[:], compare_op=ALU.not_equal, fill=1.0,
                                         base=0, pattern=[[-1, 128]], channel_multiplier=1))
            step(nc.gpsimd.tensor_copy(ident_bf[:], ident[:]))
            step(nc.gpsimd.memset(causal[:], 0.0))
            cz = causal[:].rearrange("p (h j) -> p h j", h=HC)
            for p0 in (0, PB):
                step(nc.gpsimd.affine_select(out=cz[p0:p0 + 64], in_=cz[p0:p0 + 64], compare_op=ALU.is_ge, fill=NEG,
                                             base=0, pattern=[[0, HC], [-1, S]], channel_multiplier=1))
            step(nc.gpsimd.memset(headmask[:], 1.0))
            step(nc.gpsimd.affine_select(out=headmask[:], in_=headmask[:], compare_op=ALU.is_ge, fill=0.0,
                                         base=0, pattern=[[-D, HC]], channel_multiplier=1))
            step(nc.gpsimd.affine_select(out=headmask[:], in_=headmask[:], compare_op=ALU.is_ge, fill=0.0,
                                         base=D - 1, pattern=[[D, HC]], channel_multiplier=-1))
            step(nc.gpsimd.iota(iota8i[:], pattern=[[1, NE]], base=0, channel_multiplier=0))
            step(nc.gpsimd.tensor_copy(iota8[:], iota8i[:]))
            for L in (L1, L2):
                step(nc.gpsimd.memset(L.ht[:], 0.0))
                step(nc.gpsimd.memset(L.vbd[:], 0.0))
                step(nc.gpsimd.memset(L.p[:], 0.0))
                step(nc.gpsimd.memset(L.yt[C:C + 1], 1.0))
            step(nc.gpsimd.memset(eps_col[:], EPS))
            step(nc.gpsimd.memset(hwt[:], 0.0))
            step(nc.gpsimd.memset(L2.ht[C:C + 1 + NE], 1.0))
            nc.gpsimd.memset(comb[:], 1.0).then_inc(consts_ready, 1)

            with pool.Fori(0, GROUPS) as g:
                for k in range(GT):
                    pool.wait_ge(hstage_ready, g * GT + (k + 1))
                    nc.gpsimd.tensor_copy(h_all[:, bass.ds(g * (GT * E) + k * E, E)],
                                          hstage[k % 2][:]).then_inc(hall_ready, 1)

            def take_input(t):
                if not (isinstance(t, int) and t == 0):
                    pool.wait_ge(L1.v_done, t)
                nc.gpsimd.tensor_copy(
                    L1.ht[0:C].rearrange("p c (s q) -> p c s q", s=2)[:, :, :, 0:S],
                    ht_all[:, bass.ds(t * (2 * T), 2 * T)].rearrange("p (c s j) -> p c s j", c=2, s=SEQ),
                ).then_inc(L1.ht_ready, 1)

            def block_diagonal(L, t):
                pool.wait_ge(L.k_ready, t + 1)
                if not (isinstance(t, int) and t == 0):
                    pool.wait_ge(L.scores_done, t)
                for c in range(2):
                    last = nc.gpsimd.tensor_tensor(
                        L.kbd[:, c],
                        L.kt[:, c, :].rearrange("p (s j) -> p s j", s=SEQ)[:, :, None, :].to_broadcast([C, SEQ, HC, S]),
                        headmask[:, None, :, None].to_broadcast([C, SEQ, HC, S]), ALU.mult)
                last.then_inc(L.kbd_ready, 1)

            def iteration(i, live):
                if live(0):
                    take_input(i)
                    block_diagonal(L1, i)
                if live(2):
                    block_diagonal(L2, i - 2)

            pool.wait_ge(htall_ready, TILES)
            run(pool, iteration)

        @block.tensor
        def _(pe):
            pe.wait_ge(consts_ready, 1)
            pe.wait_ge(tokw_loaded, 16)
            for n, (parts, rows, cols, dst, scale) in enumerate(prep):
                if n == TOK_PREP:
                    pe.wait_ge(weights_loaded, 16 * W_DMAS)
                if n >= 8:
                    pe.wait_ge(prep_act if n % 2 == 0 else prep_dve, (n - 8) // 2 + 1)
                for src, col in parts:
                    k = src.shape[0]
                    last = nc.tensor.transpose(ps[0:rows, n % 8, col:col + (cols if len(parts) == 1 else k)],
                                               src, ident[0:k, 0:k])
                last.then_inc(prep_tr, 1)
            pe.wait_ge(prep_act, (N_PREP + 1) // 2)
            pe.wait_ge(prep_dve, N_PREP // 2)

            def htranspose(n, k):
                pe.wait_ge(hstage_ready, n + 1)
                if k >= 2:
                    pe.wait_ge(htall_ready, n - 1)
                for c in range(2):
                    last = nc.tensor.transpose(ps[0:C, 6 + k % 2, c * T:(c + 1) * T],
                                               hstage[k % 2][:, c * C:(c + 1) * C], ident[0:T, 0:T])
                last.then_inc(htr_done, 1)

            with pe.Fori(0, GROUPS // 2) as gg:
                for u in range(2):
                    pe.wait_ge(xr_ready, gg * (2 * CH) + (u + 1) * CH)
                    for n in range(XE):
                        w, half = n // 2, n % 2
                        if n >= 4:
                            pe.wait_ge(xt_act if n % 2 == 0 else xt_dve,
                                       gg * XE + (u * WP + (n - 4) // 2 + 1))
                        for j in range(3):
                            k = half * 3 + j
                            last = nc.tensor.transpose(
                                ps[:, n % 4, j * GP:(j + 1) * GP],
                                xr[:, (k // 2) * WP + w, (k % 2) * 128:(k % 2) * 128 + 128], ident[0:GP, 0:GP])
                        last.then_inc(xtr_done, 1)
                    pe.wait_ge(xt_act, gg * XE + (u + 1) * WP)
                    pe.wait_ge(xt_dve, gg * XE + (u + 1) * WP)
                    for k in range(GT):
                        n = gg * (2 * GT) + (u * GT + k)
                        if k >= 2:
                            pe.wait_ge(hstage_ready, n - 1)
                        for kx in range(KX):
                            last = nc.tensor.matmul(ps[0:T, 4 + k % 2, 0:E], xt[:, kx, k * T:(k + 1) * T],
                                                    tokw[:, kx, :], start=(kx == 0), stop=(kx == KX - 1))
                        last.then_inc(emb_done, 1)
                        if k >= 1:
                            htranspose(gg * (2 * GT) + (u * GT + k - 1), k - 1)
                    htranspose(gg * (2 * GT) + (u * GT + GT - 1), GT - 1)
                    pe.wait_ge(htall_ready, gg * (2 * GT) + (u + 1) * GT)
            pe.wait_ge(htall_ready, TILES)

            def scores(L, t):
                at(pe, L.q_ready, t + 1)
                at(pe, L.kbd_ready, t + 1)
                at(pe, L.res_ready, t)
                for c in range(2):
                    if L is L1:
                        nc.tensor.matmul(ps[:, L.bs + c, 0:HC * S], ident_bf[:], causal[:], start=True, stop=False)
                    for s in range(SEQ):
                        last = nc.tensor.matmul(ps[s * PB:s * PB + S, L.bs + c, 0:HC * S],
                                                L.qt[:, c, s * S:(s + 1) * S],
                                                L.kbd[:, c, s].rearrange("p h j -> p (h j)"),
                                                start=(L is L2), stop=True)
                last.then_inc(L.scores_done, 1)

            def project(L, chunks, w_of, t):
                at(pe, L.q_ready, t)
                at(pe, L.k_ready, t)
                for m in range(4):
                    for n, (k, src) in enumerate(chunks):
                        last = nc.tensor.matmul(
                            ps[0:C, L.bq, m * T:(m + 1) * T], w_of(n)[0:k, m * C:(m + 1) * C],
                            src.rearrange("p (s q) -> p s q", s=2)[:, :, 0:S],
                            start=(n == 0), stop=(n == len(chunks) - 1))
                last.then_inc(L.qk_done, 1)
                at(pe, L.v_ready, t)
                for n, (k, src) in enumerate(chunks):
                    last = nc.tensor.matmul(ps[0:PP, L.bm, 0:E], src[:, 0:PP], w_of(n)[0:k, 2 * E:3 * E],
                                            start=(n == 0), stop=(n == len(chunks) - 1))
                last.then_inc(L.v_done, 1)

            def transpose_probs(L, t):
                at(pe, L.p_ready, t + 1)
                pf = L.p[:].rearrange("p h j -> p (h j)")
                for g in range(PAIRS):
                    last = nc.tensor.transpose(ps[0:PP, L.bs + g // 3, (g % 3) * PP:(g % 3 + 1) * PP],
                                               pf[:, g * 128:g * 128 + PP], ident[0:PP, 0:PP])
                last.then_inc(L.ptr_done, 1)

            def weigh_values(L, t):
                at(pe, L.pt_ready_a, t + 1)
                at(pe, L.pt_ready_b, t + 1)
                at(pe, L.v_ready, t + 1)
                for g in range(PAIRS):
                    for s in range(SEQ):
                        last = nc.tensor.matmul(
                            ps[32 * (g % 3):32 * (g % 3) + 32, L.bs, (g // 3) * T + s * S:(g // 3) * T + (s + 1) * S],
                            L.vbd[0:PP, s, 32 * g:32 * g + 32], L.pt[:, g, s * PB:s * PB + S],
                            start=True, stop=True)
                last.then_inc(L.pv_done, 1)

            def out_project(L, w, t):
                at(pe, L.yt_ready, t + 1)
                for c, k in ((0, C + 1), (1, C)):
                    last = nc.tensor.matmul(ps[0:T, L.bs + 1, 0:E], L.yt[0:k, c, :], w[0:k, c, :],
                                            start=(c == 0), stop=(c == 1))
                last.then_inc(L.proj_done, 1)

            def transpose_h1(t):
                at(pe, L1.ln_ready, t + 1)
                at(pe, L2.v_ready, t)
                for c in range(2):
                    last = nc.tensor.transpose(ps[0:C, L2.bm, c * T:(c + 1) * T], h1s[:, c * C:(c + 1) * C],
                                               ident[0:T, 0:T])
                last.then_inc(tr2_done, 1)

            def route(t):
                at(pe, L2.ht_ready, t + 1)
                for c, k in ((0, C + 1), (1, C)):
                    last = nc.tensor.matmul(ps[0:PP, L2.bm, 0:ER + NE], L2.ht[0:k, c, 0:PP],
                                            lora[0:k, c, :], start=(c == 0), stop=(c == 1))
                last.then_inc(lora_done, 1)

            def transpose_hw(t):
                at(pe, hw_ready, t + 1)
                nc.tensor.transpose(ps[0:1 + NE, L2.bm, 128:128 + PP], comb[:], ident[0:PP, 0:PP])
                nc.tensor.transpose(ps[0:ER, L2.bm, 0:PP], hw[:], ident[0:PP, 0:PP]).then_inc(hwtr_done, 1)

            chunks1 = [(C, L1.ht[0:C, 0, :]), (C, L1.ht[0:C, 1, :])]
            chunks2 = [(C + 1 + NE, L2.ht[:, 0, :]), (C, L2.ht[0:C, 1, :]), (ER, hwt[:, :])]
            w_of1 = lambda n: w1[:, n, :]
            w_of2 = lambda n: b2[:, :] if n == 2 else w2[:, n, :]

            for c in range(2):
                last = nc.tensor.matmul(ps[:, L2.bs + c, 0:HC * S], ident_bf[:], causal[:], start=True, stop=True)

            def iteration(i, live):
                a, b, c, d = i, i - 1, i - 2, i - 3
                if live(1):
                    scores(L1, b)
                if live(3):
                    scores(L2, d)
                if live(2):
                    transpose_h1(c)
                if live(0):
                    at(pe, L1.ht_ready, a + 1)
                    project(L1, chunks1, w_of1, a)
                if live(2):
                    route(c)
                if live(1):
                    transpose_probs(L1, b)
                    weigh_values(L1, b)
                if live(2):
                    transpose_hw(c)
                if live(3):
                    transpose_probs(L2, d)
                if live(1):
                    out_project(L1, p1, b)
                if live(2):
                    at(pe, hwt_ready, c + 1)
                    project(L2, chunks2, w_of2, c)
                if live(3):
                    weigh_values(L2, d)
                    out_project(L2, p2, d)

            run(pe, iteration)

        xt_view = xt[:].rearrange("p k (b h w) -> p k h b w", b=GB, h=HP)

        @block.scalar
        def _(act):
            nc.scalar.preload_act_table_set("natural_log_exp_and_others")
            act.wait_ge(consts_ready, 1)
            for n, (parts, rows, cols, dst, scale) in enumerate(prep):
                if n % 2 == 0:
                    act.wait_ge(prep_tr, n + 1)
                    src = ps[0:rows, n % 8, 0:cols]
                    if len(dst.shape) == 3:
                        src = src.rearrange("p (a b) -> p a b", a=dst.shape[1])
                    nc.scalar.activation(dst, src, ACT.Copy, scale=scale).then_inc(prep_act, 1)

            with act.Fori(0, GROUPS) as g:
                for w in range(WP):
                    act.wait_ge(xtr_done, g * XE + (2 * w + 1))
                    for j in range(3):
                        last = nc.scalar.copy(
                            xt_view[:, j, :, :, w],
                            ps[:, (2 * w) % 4, j * GP:(j + 1) * GP].rearrange("p (h b) -> p h b", h=HP))
                    last.then_inc(xt_act, 1)
                for k in range(GT):
                    act.wait_ge(emb_done, g * GT + (k + 1))
                    if k >= 2:
                        act.wait_ge(htr_done, g * GT + (k - 1))
                        act.wait_ge(hall_ready, g * GT + (k - 1))
                    nc.scalar.copy(hstage[k % 2][:], ps[0:T, 4 + k % 2, 0:E]).then_inc(hstage_ready, 1)
                act.wait_ge(htr_done, g * GT + GT)
                act.wait_ge(hall_ready, g * GT + GT)

            def exponent(L, t):
                at(act, L.sub_ready, t + 1)
                nc.scalar.activation(L.p[:, :, 0:S], L.p[:, :, 0:S], ACT.Exp).then_inc(L.exp_ready, 1)

            def take_q(L, t):
                at(act, L.qk_done, t + 1)
                at(act, L.scores_done, t)
                if L is L1:
                    for c in range(2):
                        last = nc.scalar.activation(L.qt[:, c, :], ps[0:C, L.bq, c * T:(c + 1) * T],
                                                    ACT.Identity, scale=SCALE, bias=qbias[:, c:c + 1])
                else:
                    last = nc.scalar.activation(L.qt[:].rearrange("p c t -> p (c t)"), ps[0:C, L.bq, 0:2 * T],
                                                ACT.Copy, scale=SCALE)
                last.then_inc(L.q_ready, 1)

            def take_v(L, t):
                at(act, L.v_done, t + 1)
                at(act, L.pv_done, t)
                src = ps[:, L.bm, 0:E].rearrange("p (g e d) -> p g e d", g=PAIRS, e=2)
                for s in range(SEQ):
                    dst = L.vbd[:, s, :].rearrange("p (g e d) -> p g e d", g=PAIRS, e=2)
                    for e in range(2):
                        last = nc.scalar.copy(dst[e * PB:e * PB + S, :, e, :], src[s * PB:s * PB + S, :, e, :])
                last.then_inc(L.v_ready, 1)

            def take_pt(L, t):
                at(act, L.ptr_done, t + 1)
                nc.scalar.copy(L.pt[:, 0:3, :].rearrange("p g i -> p (g i)"),
                               ps[0:PP, L.bs, 0:3 * PP]).then_inc(L.pt_ready_a, 1)

            def take_y(L, t):
                at(act, L.pv_done, t + 1)
                at(act, L.proj_done, t)
                if L is L1:
                    for c in range(2):
                        last = nc.scalar.activation(L.yt[0:C, c, :], ps[0:C, L.bs, c * T:(c + 1) * T],
                                                    ACT.Identity, bias=b6[:, 4 + c:5 + c])
                else:
                    last = nc.scalar.copy(L.yt[0:C].rearrange("p c t -> p (c t)"), ps[0:C, L.bs, 0:2 * T])
                last.then_inc(L.yt_ready, 1)

            def take_h1(t):
                at(act, tr2_done, t + 1)
                at(act, L2.v_done, t)
                nc.scalar.copy(L2.ht[0:C].rearrange("p c (s q) -> p c s q", s=2)[:, :, :, 0:S],
                               ps[0:C, L2.bm, 0:2 * T].rearrange("p (c s j) -> p c s j", c=2, s=SEQ)
                               ).then_inc(L2.ht_ready, 1)

            def router_exp(t):
                at(act, nmax_ready, t + 1)
                nc.scalar.activation(ex[:], ps[0:PP, L2.bm, ER:ER + NE], ACT.Exp, bias=nmax[:, 0:1],
                                     accum_out=esum[:, 0:1]).then_inc(ex_ready, 1)

            def take_hw(t):
                at(act, hwtr_done, t + 1)
                nc.scalar.copy(L2.ht[C:C + 1 + NE, 0, 0:PP], ps[0:1 + NE, L2.bm, 128:128 + PP])
                nc.scalar.copy(hwt[:, 0:PP], ps[0:ER, L2.bm, 0:PP]).then_inc(hwt_ready, 1)

            def inverse_deviation(L, t):
                at(act, L.mv_ready, t + 1)
                at(act, L.ln_ready, t)
                nc.scalar.activation(L.lnv[:], L.mv[:, 1:2], ACT.Ln, bias=eps_col[:, 0:1]).then_inc(L.lnv_ready, 1)
                at(act, L.lnv_ready, t + 1)
                nc.scalar.activation(L.rstd[:], L.lnv[:], ACT.Exp, scale=-0.5).then_inc(L.rstd_ready, 1)

            act.wait_ge(prep_extra, 1)

            def iteration(i, live):
                a, b, c, d = i, i - 1, i - 2, i - 3
                if live(1):
                    exponent(L1, b)
                if live(2):
                    take_h1(c)
                if live(0):
                    take_q(L1, a)
                if live(2):
                    router_exp(c)
                if live(1):
                    take_pt(L1, b)
                if live(3):
                    exponent(L2, d)
                if live(1):
                    take_y(L1, b)
                if live(2):
                    take_hw(c)
                if live(0):
                    take_v(L1, a)
                if live(3):
                    take_pt(L2, d)
                if live(1):
                    inverse_deviation(L1, b)
                if live(2):
                    take_q(L2, c)
                if live(3):
                    take_y(L2, d)
                if live(2):
                    take_v(L2, c)
                if live(3):
                    inverse_deviation(L2, d)

            run(act, iteration)

        @block.vector
        def _(dve):
            dve.wait_ge(consts_ready, 1)
            for n, (parts, rows, cols, dst, scale) in enumerate(prep):
                if n % 2 == 1:
                    dve.wait_ge(prep_tr, n + 1)
                    src = ps[0:rows, n % 8, 0:cols]
                    if len(dst.shape) == 3:
                        src = src.rearrange("p (a b) -> p a b", a=dst.shape[1])
                    if scale == 1.0:
                        last = nc.vector.tensor_copy(dst, src)
                    else:
                        last = nc.vector.tensor_scalar(dst, src, scale, None, ALU.mult)
                    last.then_inc(prep_dve, 1)
            dve.wait_ge(prep_dve, N_PREP // 2)
            dve.wait_ge(prep_act, (N_PREP + 1) // 2)
            for c in range(2):
                nc.vector.tensor_scalar(relk[:, c, :], relt[:], b6[:, 2 + c:3 + c], None, ALU.add)
            nc.vector.memset(two_rows[:], LORA_SCALE).then_inc(dve_consts, 1)
            dve.wait_ge(dve_consts, 1)
            nc.vector.memset(two_rows[0:1], 1.0).then_inc(dve_consts, 1)
            dve.wait_ge(dve_consts, 2)
            nc.vector.tensor_scalar(w2[C:C + 1 + NE, 0, :], ext_raw[:], two_rows[:, 0:1], None, ALU.mult)
            nc.vector.tensor_scalar(qbias[:], b6[:, 0:2], SCALE, None, ALU.mult).then_inc(prep_extra, 1)
            dve.wait_ge(prep_extra, 1)

            def regroup(u, loaded):
                dve.wait_ge(x_loaded[u], loaded)
                for ch in range(CH):
                    nc.vector.tensor_copy(
                        xr[:, ch * WP:(ch + 1) * WP, :].rearrange("p w (q v) -> p q w v", q=PATCH),
                        xb[u][:, ch, :].rearrange("p (q w v) -> p q w v", q=PATCH, w=WP)).then_inc(xr_ready, 1)

            with dve.Fori(0, GROUPS // 2) as gg:
                for u in range(2):
                    regroup(u, gg * (16 * HP) + 16 * HP)
                    for w in range(WP):
                        dve.wait_ge(xtr_done, gg * (2 * XE) + (u * XE + 2 * w + 2))
                        for j in range(3):
                            last = nc.vector.tensor_copy(
                                xt_view[:, 3 + j, :, :, w],
                                ps[:, (2 * w + 1) % 4, j * GP:(j + 1) * GP].rearrange("p (h b) -> p h b", h=HP))
                        last.then_inc(xt_dve, 1)
                    for k in range(GT):
                        dve.wait_ge(htr_done, gg * (2 * GT) + (u * GT + k + 1))
                        nc.vector.tensor_copy(
                            ht_all[:, bass.ds(gg * (2 * GT * 2 * T) + (u * GT + k) * 2 * T, 2 * T)],
                            ps[0:C, 6 + k % 2, 0:2 * T]).then_inc(htall_ready, 1)
                    dve.wait_ge(emb_done, gg * (2 * GT) + (u + 1) * GT)
            dve.wait_ge(hall_ready, TILES)

            def score_view(L):
                return ps[0:PP, L.bs:L.bs + 2, 0:HC * S].rearrange("p b (h j) -> p b h j", h=HC)

            def probs_view(L):
                return L.p[:, :, 0:S].rearrange("p (b h) j -> p b h j", b=2)

            def subtract_max(L, t):
                at(dve, L.scores_done, t + 1)
                nc.vector.tensor_reduce(L.mx[:].rearrange("p (b h) -> p b h", b=2), score_view(L), AX.X,
                                        ALU.max).then_inc(L.mx_ready, 1)
                at(dve, L.mx_ready, t + 1)
                at(dve, L.ptr_done, t)
                nc.vector.tensor_tensor(
                    probs_view(L), score_view(L),
                    L.mx[:].rearrange("p (b h) -> p b h", b=2)[:, :, :, None].to_broadcast([PP, 2, HC, S]),
                    ALU.subtract).then_inc(L.sub_ready, 1)

            def normalise(L, t):
                at(dve, L.exp_ready, t + 1)
                nc.vector.tensor_reduce(L.sum[:], L.p[:, :, 0:S], AX.X, ALU.add).then_inc(L.sum_ready, 1)
                at(dve, L.sum_ready, t + 1)
                nc.vector.reciprocal(L.rsum[:], L.sum[:]).then_inc(L.rsum_ready, 1)
                at(dve, L.rsum_ready, t + 1)
                nc.vector.tensor_tensor(L.p[:, :, 0:S], L.p[:, :, 0:S],
                                        L.rsum[:, :, None].to_broadcast([PP, H, S]),
                                        ALU.mult).then_inc(L.p_ready, 1)

            def take_k(L, t):
                at(dve, L.q_ready, t + 1)
                at(dve, L.kbd_ready, t)
                src = ps[0:C, L.bq, 2 * T:4 * T].rearrange("p (c s j) -> p c s j", c=2, s=SEQ)
                if L is L1:
                    last = nc.vector.tensor_tensor(
                        L.kt[:].rearrange("p c (s j) -> p c s j", s=SEQ), src,
                        relk[:, :, None, :].to_broadcast([C, 2, SEQ, S]), ALU.add)
                else:
                    last = nc.vector.tensor_copy(L.kt[:].rearrange("p c (s j) -> p c s j", s=SEQ), src)
                last.then_inc(L.k_ready, 1)

            def take_pt(L, t):
                at(dve, L.ptr_done, t + 1)
                nc.vector.tensor_copy(L.pt[:, 3:6, :].rearrange("p g i -> p (g i)"),
                                      ps[0:PP, L.bs + 1, 0:3 * PP]).then_inc(L.pt_ready_b, 1)

            def layernorm(L, t):
                at(dve, L.proj_done, t + 1)
                if not (isinstance(t, int) and t == 0) and L is L2:
                    at(dve, h1_kept, t + 1)
                nc.vector.tensor_tensor(L.res[:], ps[0:T, L.bs + 1, 0:E], h_all[:, bass.ds(t * E, E)],
                                        ALU.add).then_inc(L.res_ready, 1)
                at(dve, L.res_ready, t + 1)
                nc.vector.bn_stats(L.st[:], L.res[:]).then_inc(L.st_ready, 1)
                at(dve, L.st_ready, t + 1)
                nc.vector.memset(L.pad[:], 0.0)
                nc.vector.bn_aggr(L.mv[:], L.st[:]).then_inc(L.mv_ready, 1)
                at(dve, L.rstd_ready, t + 1)
                if L is L1:
                    at(dve, tr2_done, t)
                    nc.vector.tensor_scalar(h1s[:], L.res[:], L.mv[:, 0:1], L.rstd[:, 0:1], ALU.subtract,
                                            ALU.mult).then_inc(L.ln_ready, 1)
                    nc.vector.tensor_scalar(h_all[:, bass.ds(t * E, E)], L.res[:], L.mv[:, 0:1], L.rstd[:, 0:1],
                                            ALU.subtract, ALU.mult).then_inc(h1_kept, 1)
                else:
                    at(dve, out_stored, t * 16)
                    nc.vector.tensor_scalar(o_sb[:], L.res[:], L.mv[:, 0:1], L.rstd[:, 0:1], ALU.subtract,
                                            ALU.mult).then_inc(L.ln_ready, 1)

            def router_max(t):
                at(dve, lora_done, t + 1)
                nc.vector.tensor_reduce(nmax[:], ps[0:PP, L2.bm, ER:ER + NE], AX.X, ALU.max,
                                        negate=True).then_inc(nmax_ready, 1)

            RS = 5

            def combine(t):
                def step(ins, k):
                    ins.then_inc(router_step, 1)
                    at(dve, router_step, t * RS + k)

                at(dve, ex_ready, t + 1)
                nc.vector.reciprocal(resum[:], esum[:])
                step(nc.vector.max(top8[:], ex[:]), 1)
                nc.vector.tensor_scalar(en[:], ex[:], resum[:, 0:1], None, ALU.mult)
                step(nc.vector.max_index(idx8[:], top8[:], ex[:]), 2)
                step(nc.vector.tensor_copy(idxf[:], idx8[:, 0:2]), 3)
                nc.vector.scalar_tensor_tensor(out=pick0[:], in0=iota8[:], scalar=idxf[:, 0:1], in1=en[:],
                                               op0=ALU.is_equal, op1=ALU.mult)
                step(nc.vector.scalar_tensor_tensor(out=pick1[:], in0=iota8[:], scalar=idxf[:, 1:2], in1=en[:],
                                                    op0=ALU.is_equal, op1=ALU.mult), 4)
                step(nc.vector.tensor_tensor(comb[:, 1:1 + NE], pick0[:], pick1[:], ALU.add), 5)
                nc.vector.tensor_tensor(
                    hw[:].rearrange("p (e r) -> p e r", e=NE),
                    ps[0:PP, L2.bm, 0:ER].rearrange("p (e r) -> p e r", e=NE),
                    comb[:, 1:1 + NE][:, :, None].to_broadcast([PP, NE, R]), ALU.mult).then_inc(hw_ready, 1)

            def iteration(i, live):
                a, b, c, d = i, i - 1, i - 2, i - 3
                if live(1):
                    subtract_max(L1, b)
                    normalise(L1, b)
                if live(0):
                    take_k(L1, a)
                if live(3):
                    subtract_max(L2, d)
                if live(2):
                    router_max(c)
                if live(1):
                    take_pt(L1, b)
                if live(2):
                    combine(c)
                if live(3):
                    normalise(L2, d)
                if live(1):
                    layernorm(L1, b)
                if live(3):
                    take_pt(L2, d)
                if live(2):
                    take_k(L2, c)
                if live(3):
                    layernorm(L2, d)

            run(dve, iteration)


_INS = ['x', 'L0_tok_W', 'L0_attn_w_attn', 'L0_attn_b_attn', 'L0_attn_w_proj', 'L0_attn_b_proj', 'L0_attn_rel_emb',
        'L0_ffn_Wg', 'L0_ffn_bg', 'L0_ffn_Wqkv', 'L0_ffn_bqkv', 'L0_ffn_Wproj', 'L0_ffn_bproj', 'L0_ffn_A',
        'L0_ffn_ba', 'L0_ffn_Bm', 'L0_ffn_bb']
_OUT = ((64, 49, 192), 'float32')


def kernel(**inputs):
    import numpy as _np
    import concourse.bacc as _bacc
    from concourse import mybir as _mybir
    from concourse.bass_utils import run_bass_kernel_spmd as _run

    nc = _bacc.Bacc("TRN2", target_bir_lowering=False, num_devices=1)
    arrays, args = {}, []
    for name in _INS:
        a = _np.ascontiguousarray(inputs[name])
        arrays[f"in_{name}"] = a
        args.append(nc.dram_tensor(f"in_{name}", a.shape, _mybir.dt.from_np(a.dtype), kind="ExternalInput").ap())
    args.append(nc.dram_tensor("out_0", _OUT[0], _mybir.dt.from_np(_np.dtype(_OUT[1])), kind="ExternalOutput").ap())
    build(nc, *args)
    r = _run(nc, [arrays], core_ids=[0])
    return r.results[0]["out_0"]
```

```python
from contextlib import ExitStack

import concourse.bass as bass
from concourse import mybir

F32 = mybir.dt.float32
BF16 = mybir.dt.bfloat16
U32 = mybir.dt.uint32
ALU = mybir.AluOpType
ACT = mybir.ActivationFunctionType
AX = mybir.AxisListType


def build(nc, x, tok_w, w_attn, b_attn, w_proj, b_proj, rel_emb, wg, bg, wqkv, bqkv, wproj2, bproj2,
          lora_a, lora_ba, lora_b, lora_bb, out):
    NB, CH, HI, WI = x.shape
    E, PD = tok_w.shape
    PATCH = 16
    HP, WP = HI // PATCH, WI // PATCH
    S = HP * WP
    SEQ = 2
    T = SEQ * S
    TILES = NB // SEQ
    GB = 16
    GROUPS = NB // GB
    GT = GB // SEQ
    GP = HP * GB
    H = 12
    D = E // H
    C = E // 2
    HC = H // 2
    KX = PD // 128
    NE, R, _ = lora_a.shape
    ER = NE * R
    QKV = 3 * E
    PB = 64
    PP = PB + S
    PAIRS = H // 2
    SCALE = float(D) ** -0.5
    LORA_SCALE = 32 / R
    EPS = 1e-5
    NEG = -1e30
    assert PD == KX * 128 and S <= PB and D * 2 == 32 and ER == 128 and 6 * 98 == H * S

    with ExitStack() as ctx:
        def sb(name, shape, dt=F32):
            return ctx.enter_context(nc.sbuf_tensor(name, shape, dt))

        def sem(name):
            return ctx.enter_context(nc.semaphore(name))

        ps = ctx.enter_context(nc.psum_tensor("ps", [128, 8, 512], F32))

        ident = sb("ident", [128, 128])
        ident_bf = sb("ident_bf", [128, 128], BF16)
        causal = sb("causal", [128, HC * S], BF16)
        headmask = sb("headmask", [C, HC])
        iota8i = sb("iota8i", [PP, NE], mybir.dt.int32)
        iota8 = sb("iota8", [PP, NE])
        eps_col = sb("eps_col", [T, 1])
        two_rows = sb("two_rows", [1 + NE, 1])

        tokw_raw = sb("tokw_raw", [C, 2, PD])
        xr = sb("xr", [GP, CH * WP, PATCH * PATCH])
        xr_flat = xr[0:C].rearrange("p a b -> p (a b)")
        wqkv_raw = xr_flat[:, 0:6 * E].rearrange("p (m k) -> p m k", m=6)
        wproj_raw = xr_flat[:, 6 * E:8 * E].rearrange("p (m k) -> p m k", m=2)
        bm_raw = xr_flat[:, 8 * E:8 * E + 6 * ER].rearrange("p (m e r) -> p m e r", m=6, e=NE)
        a_raw = sb("a_raw", [ER, E])
        g_raw = sb("g_raw", [NE, E])
        b6_raw = sb("b6_raw", [6, C])
        rel_raw = sb("rel_raw", [S, HC, D])
        ext_raw = sb("ext_raw", [1 + NE, QKV])
        tokw = sb("tokw", [128, KX, E])
        w1 = sb("w1", [C, 2, QKV])
        p1 = sb("p1", [C + 1, 2, E])
        b6 = sb("b6", [C, 6])
        qbias = sb("qbias", [C, 2])
        relt = sb("relt", [C, S])
        relk = sb("relk", [C, 2, S])
        w2 = sb("w2", [C + 1 + NE, 2, QKV])
        b2 = sb("b2", [ER, QKV])
        p2 = sb("p2", [C + 1, 2, E])
        lora = sb("lora", [C + 1, 2, ER + NE])

        xb = [sb(f"xb{u}", [GP, CH, PATCH * WI]) for u in range(2)]
        xt = sb("xt", [128, KX, GB * S])
        hstage = [sb(f"hstage{u}", [T, E]) for u in range(2)]
        h_all = sb("h_all", [T, TILES * E])
        ht_all = sb("ht_all", [C, TILES * 2 * T])

        class Layer:

            def __init__(self, n, bank):
                self.bq, self.bm, self.bs = bank, bank + 1, bank + 2
                self.ht = sb(f"ht{n}", [C + 1 + NE, 2, 128])
                self.qk = sb(f"qk{n}", [C, 4, T])
                self.qt, self.kt = self.qk[:, 0:2, :], self.qk[:, 2:4, :]
                self.kbd = sb(f"kbd{n}", [C, 2, SEQ, HC, S])
                self.vbd = sb(f"vbd{n}", [128, SEQ, E])
                self.mx = sb(f"mx{n}", [PP, H])
                self.p = sb(f"probs{n}", [PP, H, 64])
                self.sum = sb(f"sum{n}", [PP, H])
                self.rsum = sb(f"rsum{n}", [PP, H])
                self.pt = sb(f"pt{n}", [PP, PAIRS, PP])
                self.yt = sb(f"yt{n}", [C + 1, 2, T])
                self.res = sb(f"res{n}", [T, E])
                self.st = sb(f"st{n}", [T, 6])
                self.pad = sb(f"pad{n}", [1, 1])
                self.mv = sb(f"mv{n}", [T, 2])
                self.lnv = sb(f"lnv{n}", [T, 1])
                self.rstd = sb(f"rstd{n}", [T, 1])
                self.ht_ready = sem(f"ht_ready{n}")
                self.qk_done = sem(f"qk_done{n}")
                self.v_done = sem(f"v_done{n}")
                self.q_ready = sem(f"q_ready{n}")
                self.k_ready = sem(f"k_ready{n}")
                self.kbd_ready = sem(f"kbd_ready{n}")
                self.v_ready = sem(f"v_ready{n}")
                self.scores_done = sem(f"scores_done{n}")
                self.mx_ready = sem(f"mx_ready{n}")
                self.sub_ready = sem(f"sub_ready{n}")
                self.exp_ready = sem(f"exp_ready{n}")
                self.sum_ready = sem(f"sum_ready{n}")
                self.rsum_ready = sem(f"rsum_ready{n}")
                self.p_ready = sem(f"p_ready{n}")
                self.ptr_done = sem(f"ptr_done{n}")
                self.pt_ready_a = sem(f"pt_ready_a{n}")
                self.pt_ready_b = sem(f"pt_ready_b{n}")
                self.pv_done = sem(f"pv_done{n}")
                self.yt_ready = sem(f"yt_ready{n}")
                self.proj_done = sem(f"proj_done{n}")
                self.res_ready = sem(f"res_ready{n}")
                self.st_ready = sem(f"st_ready{n}")
                self.mv_ready = sem(f"mv_ready{n}")
                self.lnv_ready = sem(f"lnv_ready{n}")
                self.rstd_ready = sem(f"rstd_ready{n}")
                self.ln_ready = sem(f"ln_ready{n}")

        L1 = Layer(1, 0)
        L2 = Layer(2, 4)
        L2.q_ready = L2.k_ready
        h1s = sb("h1s", [T, E])
        o_sb = sb("o_sb", [T, E])
        hwt = sb("hwt", [ER, 128])
        nmax = sb("nmax", [PP, 1])
        ex = sb("ex", [PP, NE])
        esum = sb("esum", [PP, 1])
        resum = sb("resum", [PP, 1])
        top8 = sb("top8", [PP, 8])
        idx8 = sb("idx8", [PP, 8], U32)
        en = sb("en", [PP, NE])
        pick0 = sb("pick0", [PP, NE])
        pick1 = sb("pick1", [PP, NE])
        comb = sb("comb", [PP, 1 + NE])
        hw = sb("hw", [PP, ER])

        tokw_loaded = sem("tokw_loaded")
        weights_loaded = sem("weights_loaded")
        x_loaded = [sem(f"x_loaded{u}") for u in range(2)]
        rel_zeroed = sem("rel_zeroed")
        pool_step = sem("pool_step")
        consts_ready = sem("consts_ready")
        dve_consts = sem("dve_consts")
        prep_tr = sem("prep_tr")
        prep_act = sem("prep_act")
        prep_dve = sem("prep_dve")
        prep_extra = sem("prep_extra")
        xr_ready = sem("xr_ready")
        xtr_done = sem("xtr_done")
        xt_act = sem("xt_act")
        xt_dve = sem("xt_dve")
        emb_done = sem("emb_done")
        hstage_ready = sem("hstage_ready")
        htr_done = sem("htr_done")
        htall_ready = sem("htall_ready")
        hall_ready = sem("hall_ready")
        tr2_done = sem("tr2_done")
        lora_done = sem("lora_done")
        nmax_ready = sem("nmax_ready")
        ex_ready = sem("ex_ready")
        router_step = sem("router_step")
        hw_ready = sem("hw_ready")
        hwtr_done = sem("hwtr_done")
        hwt_ready = sem("hwt_ready")
        h1_kept = sem("h1_kept")
        out_stored = sem("out_stored")

        W_DMAS = 27

        prep = []
        for half in range(2):
            for k in range(0, KX, 3):
                prep.append(([(tokw_raw[:, half, (k + j) * 128:(k + j + 1) * 128], j * C) for j in range(3)],
                             128, 3 * C, tokw[:, k:k + 3, half * C:(half + 1) * C], 1.0))
        TOK_PREP = len(prep)
        for kc in range(2):
            for m in range(0, 6, 3):
                prep.append(([(wqkv_raw[:, m + j, kc * C:(kc + 1) * C], j * C) for j in range(3)],
                             C, 3 * C, w2[0:C, kc, m * C:(m + 3) * C], 1.0))
        for m in range(0, 6, 3):
            prep.append(([(bm_raw[:, m + j, :, :].rearrange("p e r -> p (e r)"), j * C) for j in range(3)],
                         ER, 3 * C, b2[:, m * C:(m + 3) * C], LORA_SCALE))
        for kc in range(2):
            prep.append(([(wproj_raw[:, j, kc * C:(kc + 1) * C], j * C) for j in range(2)],
                         C, 2 * C, p2[0:C, kc, :], 1.0))
            prep.append(([(a_raw[:, kc * C:(kc + 1) * C], 0), (g_raw[:, kc * C:(kc + 1) * C], ER)],
                         C, ER + NE, lora[0:C, kc, :], 1.0))
        prep.append(([(b6_raw[:, :], 0)], C, 6, b6[:, :], 1.0))
        prep.append(([(rel_raw[:, :, :].rearrange("p h d -> p (h d)"), 0)], C, S, relt[:, :], 1.0))
        N_PREP = len(prep)
        XE = 2 * WP

        STAGES = 5

        def run(eng, iteration):
            for i in range(STAGES):
                iteration(i, lambda s, i=i: i >= s)
            with eng.Fori(STAGES, TILES) as i:
                iteration(i, lambda s: True)
            for i in range(TILES, TILES + STAGES - 1):
                iteration(i, lambda s, i=i: i - s < TILES)

        def at(eng, semaphore, n):
            if not (isinstance(n, int) and n <= 0):
                eng.wait_ge(semaphore, n)

        block = ctx.enter_context(nc.Block())

        @block.sync
        def _(sp):
            def load_x(g):
                src = x[g * GB:(g + 1) * GB].rearrange("b c (h q) w -> h b c (q w)", q=PATCH)
                for hp in range(HP):
                    sp.dma_start(xb[g % 2][hp * GB:(hp + 1) * GB], src[hp]).then_inc(x_loaded[g % 2], 16)

            sp.dma_start(tokw_raw[:], tok_w.rearrange("(h p) k -> p h k", p=C)).then_inc(tokw_loaded, 16)
            load_x(0)

            def load_w(dst, src):
                sp.dma_start(dst, src).then_inc(weights_loaded, 16)

            load_w(w1[:], w_attn.rearrange("(k p) n -> p k n", p=C))
            load_w(p1[0:C], w_proj.rearrange("(k p) n -> p k n", p=C))
            load_w(p1[C:C + 1, 0, :], b_proj.unsqueeze(0))
            load_w(b6_raw[:], b_attn.rearrange("(m p) -> m p", p=C))
            sp.wait_ge(rel_zeroed, 1)
            for h in range(HC):
                load_w(rel_raw[1:S, h, :], rel_emb[0:S - 1])
            load_w(wqkv_raw, wqkv.rearrange("(m p) k -> p m k", p=C))
            load_w(ext_raw[0:1], bqkv.unsqueeze(0))
            load_w(ext_raw[1:1 + NE], lora_bb)
            load_w(wproj_raw, wproj2.rearrange("(m p) k -> p m k", p=C))
            load_w(p2[C:C + 1, 0, :], bproj2.unsqueeze(0))
            load_w(a_raw[:], lora_a.rearrange("e r k -> (e r) k"))
            load_w(g_raw[:], wg)
            load_w(lora[C:C + 1, 0, 0:ER], lora_ba.rearrange("e r -> (e r)").unsqueeze(0))
            load_w(lora[C:C + 1, 0, ER:ER + NE], bg.unsqueeze(0))
            for e in range(NE):
                load_w(bm_raw[:, :, e, :], lora_b[e].rearrange("(m p) r -> p m r", p=C))
            load_x(1)
            for g in range(2, GROUPS):
                sp.wait_ge(xr_ready, CH * (g - 1))
                load_x(g)

            out_rows = out.rearrange("b n e -> (b n) e")
            with sp.Fori(0, TILES) as t:
                sp.wait_ge(L2.ln_ready, t + 1)
                sp.dma_start(out_rows[bass.ds(t * T, T)], o_sb[:]).then_inc(out_stored, 16)
            sp.wait_ge(out_stored, 16 * TILES)

        @block.gpsimd
        def _(pool):
            steps = [0]

            def step(ins):
                steps[0] += 1
                ins.then_inc(pool_step, 1)
                pool.wait_ge(pool_step, steps[0])

            nc.gpsimd.memset(rel_raw[:], 0.0).then_inc(rel_zeroed, 1)
            step(nc.gpsimd.memset(ident[:], 0.0))
            step(nc.gpsimd.affine_select(out=ident[:], in_=ident[:], compare_op=ALU.not_equal, fill=1.0,
                                         base=0, pattern=[[-1, 128]], channel_multiplier=1))
            step(nc.gpsimd.tensor_copy(ident_bf[:], ident[:]))
            step(nc.gpsimd.memset(causal[:], 0.0))
            cz = causal[:].rearrange("p (h j) -> p h j", h=HC)
            for p0 in (0, PB):
                step(nc.gpsimd.affine_select(out=cz[p0:p0 + 64], in_=cz[p0:p0 + 64], compare_op=ALU.is_ge, fill=NEG,
                                             base=0, pattern=[[0, HC], [-1, S]], channel_multiplier=1))
            step(nc.gpsimd.memset(headmask[:], 1.0))
            step(nc.gpsimd.affine_select(out=headmask[:], in_=headmask[:], compare_op=ALU.is_ge, fill=0.0,
                                         base=0, pattern=[[-D, HC]], channel_multiplier=1))
            step(nc.gpsimd.affine_select(out=headmask[:], in_=headmask[:], compare_op=ALU.is_ge, fill=0.0,
                                         base=D - 1, pattern=[[D, HC]], channel_multiplier=-1))
            step(nc.gpsimd.iota(iota8i[:], pattern=[[1, NE]], base=0, channel_multiplier=0))
            step(nc.gpsimd.tensor_copy(iota8[:], iota8i[:]))
            for L in (L1, L2):
                step(nc.gpsimd.memset(L.ht[:], 0.0))
                step(nc.gpsimd.memset(L.vbd[:], 0.0))
                step(nc.gpsimd.memset(L.p[:], 0.0))
                step(nc.gpsimd.memset(L.yt[C:C + 1], 1.0))
            step(nc.gpsimd.memset(eps_col[:], EPS))
            step(nc.gpsimd.memset(hwt[:], 0.0))
            step(nc.gpsimd.memset(L2.ht[C:C + 1 + NE], 1.0))
            nc.gpsimd.memset(comb[:], 1.0).then_inc(consts_ready, 1)

            with pool.Fori(0, GROUPS) as g:
                for k in range(GT):
                    pool.wait_ge(hstage_ready, g * GT + (k + 1))
                    nc.gpsimd.tensor_copy(h_all[:, bass.ds(g * (GT * E) + k * E, E)],
                                          hstage[k % 2][:]).then_inc(hall_ready, 1)

            def take_input(t):
                if not (isinstance(t, int) and t == 0):
                    pool.wait_ge(L1.v_done, t)
                nc.gpsimd.tensor_copy(
                    L1.ht[0:C].rearrange("p c (s q) -> p c s q", s=2)[:, :, :, 0:S],
                    ht_all[:, bass.ds(t * (2 * T), 2 * T)].rearrange("p (c s j) -> p c s j", c=2, s=SEQ),
                ).then_inc(L1.ht_ready, 1)

            def block_diagonal(L, t):
                pool.wait_ge(L.k_ready, t + 1)
                if not (isinstance(t, int) and t == 0):
                    pool.wait_ge(L.scores_done, t)
                for c in range(2):
                    last = nc.gpsimd.tensor_tensor(
                        L.kbd[:, c],
                        L.kt[:, c, :].rearrange("p (s j) -> p s j", s=SEQ)[:, :, None, :].to_broadcast([C, SEQ, HC, S]),
                        headmask[:, None, :, None].to_broadcast([C, SEQ, HC, S]), ALU.mult)
                last.then_inc(L.kbd_ready, 1)

            def keep_h1(t):
                pool.wait_ge(L1.ln_ready, t + 1)
                nc.gpsimd.tensor_copy(h_all[:, bass.ds(t * E, E)], h1s[:]).then_inc(h1_kept, 1)

            def iteration(i, live):
                if live(0):
                    take_input(i)
                    block_diagonal(L1, i)
                if live(1):
                    keep_h1(i - 1)
                if live(2):
                    block_diagonal(L2, i - 2)

            pool.wait_ge(htall_ready, TILES)
            run(pool, iteration)

        @block.tensor
        def _(pe):
            pe.wait_ge(consts_ready, 1)
            pe.wait_ge(tokw_loaded, 16)
            for n, (parts, rows, cols, dst, scale) in enumerate(prep):
                if n == TOK_PREP:
                    pe.wait_ge(weights_loaded, 16 * W_DMAS)
                if n >= 8:
                    pe.wait_ge(prep_act if n % 2 == 0 else prep_dve, (n - 8) // 2 + 1)
                for src, col in parts:
                    k = src.shape[0]
                    last = nc.tensor.transpose(ps[0:rows, n % 8, col:col + (cols if len(parts) == 1 else k)],
                                               src, ident[0:k, 0:k])
                last.then_inc(prep_tr, 1)
            pe.wait_ge(prep_act, (N_PREP + 1) // 2)
            pe.wait_ge(prep_dve, N_PREP // 2)

            def htranspose(n, k):
                pe.wait_ge(hstage_ready, n + 1)
                if k >= 2:
                    pe.wait_ge(htall_ready, n - 1)
                for c in range(2):
                    last = nc.tensor.transpose(ps[0:C, 6 + k % 2, c * T:(c + 1) * T],
                                               hstage[k % 2][:, c * C:(c + 1) * C], ident[0:T, 0:T])
                last.then_inc(htr_done, 1)

            with pe.Fori(0, GROUPS // 2) as gg:
                for u in range(2):
                    pe.wait_ge(xr_ready, gg * (2 * CH) + (u + 1) * CH)
                    for n in range(XE):
                        w, half = n // 2, n % 2
                        if n >= 4:
                            pe.wait_ge(xt_act if n % 2 == 0 else xt_dve,
                                       gg * XE + (u * WP + (n - 4) // 2 + 1))
                        for j in range(3):
                            k = half * 3 + j
                            last = nc.tensor.transpose(
                                ps[:, n % 4, j * GP:(j + 1) * GP],
                                xr[:, (k // 2) * WP + w, (k % 2) * 128:(k % 2) * 128 + 128], ident[0:GP, 0:GP])
                        last.then_inc(xtr_done, 1)
                    pe.wait_ge(xt_act, gg * XE + (u + 1) * WP)
                    pe.wait_ge(xt_dve, gg * XE + (u + 1) * WP)
                    for k in range(GT):
                        n = gg * (2 * GT) + (u * GT + k)
                        if k >= 2:
                            pe.wait_ge(hstage_ready, n - 1)
                        for kx in range(KX):
                            last = nc.tensor.matmul(ps[0:T, 4 + k % 2, 0:E], xt[:, kx, k * T:(k + 1) * T],
                                                    tokw[:, kx, :], start=(kx == 0), stop=(kx == KX - 1))
                        last.then_inc(emb_done, 1)
                        if k >= 1:
                            htranspose(gg * (2 * GT) + (u * GT + k - 1), k - 1)
                    htranspose(gg * (2 * GT) + (u * GT + GT - 1), GT - 1)
                    pe.wait_ge(htall_ready, gg * (2 * GT) + (u + 1) * GT)
            pe.wait_ge(htall_ready, TILES)
            pe.wait_ge(prep_extra, 4)

            def scores(L, t):
                at(pe, L.q_ready, t + 1)
                at(pe, L.kbd_ready, t + 1)
                at(pe, L.res_ready, t)
                for c in range(2):
                    if L is L1:
                        nc.tensor.matmul(ps[:, L.bs + c, 0:HC * S], ident_bf[:], causal[:], start=True, stop=False)
                    for s in range(SEQ):
                        last = nc.tensor.matmul(ps[s * PB:s * PB + S, L.bs + c, 0:HC * S],
                                                L.qt[:, c, s * S:(s + 1) * S],
                                                L.kbd[:, c, s].rearrange("p h j -> p (h j)"),
                                                start=(L is L2), stop=True)
                last.then_inc(L.scores_done, 1)

            def project_qk(L, chunks, w_of, t):
                at(pe, L.q_ready, t)
                at(pe, L.k_ready, t)
                for m in range(4):
                    for n, (k, src) in enumerate(chunks):
                        last = nc.tensor.matmul(
                            ps[0:C, L.bq, m * T:(m + 1) * T], w_of(n)[0:k, m * C:(m + 1) * C],
                            src.rearrange("p (s q) -> p s q", s=2)[:, :, 0:S],
                            start=(n == 0), stop=(n == len(chunks) - 1))
                last.then_inc(L.qk_done, 1)

            def project_v(L, chunks, w_of, t):
                at(pe, L.v_ready, t)
                for n, (k, src) in enumerate(chunks):
                    last = nc.tensor.matmul(ps[0:PP, L.bm, 0:E], src[:, 0:PP], w_of(n)[0:k, 2 * E:3 * E],
                                            start=(n == 0), stop=(n == len(chunks) - 1))
                last.then_inc(L.v_done, 1)

            def transpose_probs(L, t):
                at(pe, L.p_ready, t + 1)
                pf = L.p[:].rearrange("p h j -> p (h j)")
                for g in range(PAIRS):
                    last = nc.tensor.transpose(ps[0:PP, L.bs + g // 3, (g % 3) * PP:(g % 3 + 1) * PP],
                                               pf[:, g * 128:g * 128 + PP], ident[0:PP, 0:PP])
                last.then_inc(L.ptr_done, 1)

            def weigh_values(L, t):
                at(pe, L.v_ready, t + 1)
                for g in range(PAIRS):
                    if g % 3 == 0:
                        at(pe, L.pt_ready_b if g else L.pt_ready_a, t + 1)
                    for s in range(SEQ):
                        last = nc.tensor.matmul(
                            ps[32 * (g % 3):32 * (g % 3) + 32, L.bs, (g // 3) * T + s * S:(g // 3) * T + (s + 1) * S],
                            L.vbd[0:PP, s, 32 * g:32 * g + 32], L.pt[:, g, s * PB:s * PB + S],
                            start=True, stop=True)
                last.then_inc(L.pv_done, 1)

            def out_project(L, w, t):
                at(pe, L.yt_ready, t + 1)
                for c, k in ((0, C + 1), (1, C)):
                    last = nc.tensor.matmul(ps[0:T, L.bs + 1, 0:E], L.yt[0:k, c, :], w[0:k, c, :],
                                            start=(c == 0), stop=(c == 1))
                last.then_inc(L.proj_done, 1)

            def transpose_h1(t):
                at(pe, L1.ln_ready, t + 1)
                if not (isinstance(t, int) and t + 2 > TILES):
                    at(pe, L1.v_ready, t + 2)
                for c in range(2):
                    last = nc.tensor.transpose(ps[0:C, L1.bm, c * T:(c + 1) * T], h1s[:, c * C:(c + 1) * C],
                                               ident[0:T, 0:T])
                last.then_inc(tr2_done, 1)

            def route(t):
                at(pe, L2.ht_ready, t + 1)
                at(pe, L2.v_ready, t)
                for c, k in ((0, C + 1), (1, C)):
                    last = nc.tensor.matmul(ps[0:PP, L2.bm, 0:ER + NE], L2.ht[0:k, c, 0:PP],
                                            lora[0:k, c, :], start=(c == 0), stop=(c == 1))
                last.then_inc(lora_done, 1)

            def transpose_hw(t):
                at(pe, hw_ready, t + 1)
                nc.tensor.transpose(ps[0:1 + NE, L2.bm, 128:128 + PP], comb[:], ident[0:PP, 0:PP])
                nc.tensor.transpose(ps[0:ER, L2.bm, 0:PP], hw[:], ident[0:PP, 0:PP]).then_inc(hwtr_done, 1)

            chunks1 = [(C, L1.ht[0:C, 0, :]), (C, L1.ht[0:C, 1, :])]
            chunks2 = [(C + 1 + NE, L2.ht[:, 0, :]), (C, L2.ht[0:C, 1, :]), (ER, hwt[:, :])]
            w_of1 = lambda n: w1[:, n, :]
            w_of2 = lambda n: b2[:, :] if n == 2 else w2[:, n, :]

            for c in range(2):
                last = nc.tensor.matmul(ps[:, L2.bs + c, 0:HC * S], ident_bf[:], causal[:], start=True, stop=True)

            def iteration(i, live):
                a, b, c, d, e = i, i - 1, i - 2, i - 3, i - 4
                if live(2):
                    transpose_h1(c)
                if live(4):
                    weigh_values(L2, e)
                if live(1):
                    scores(L1, b)
                if live(4):
                    out_project(L2, p2, e)
                if live(2):
                    route(c)
                if live(0):
                    at(pe, L1.ht_ready, a + 1)
                    project_qk(L1, chunks1, w_of1, a)
                if live(3):
                    scores(L2, d)
                if live(1):
                    transpose_probs(L1, b)
                if live(0):
                    project_v(L1, chunks1, w_of1, a)
                if live(1):
                    weigh_values(L1, b)
                if live(2):
                    transpose_hw(c)
                if live(1):
                    out_project(L1, p1, b)
                if live(2):
                    at(pe, hwt_ready, c + 1)
                    project_qk(L2, chunks2, w_of2, c)
                    project_v(L2, chunks2, w_of2, c)
                if live(3):
                    transpose_probs(L2, d)

            run(pe, iteration)

        xt_view = xt[:].rearrange("p k (b h w) -> p k h b w", b=GB, h=HP)

        @block.scalar
        def _(act):
            nc.scalar.preload_act_table_set("natural_log_exp_and_others")
            act.wait_ge(consts_ready, 1)
            for n, (parts, rows, cols, dst, scale) in enumerate(prep):
                if n % 2 == 0:
                    act.wait_ge(prep_tr, n + 1)
                    src = ps[0:rows, n % 8, 0:cols]
                    if len(dst.shape) == 3:
                        src = src.rearrange("p (a b) -> p a b", a=dst.shape[1])
                    nc.scalar.activation(dst, src, ACT.Copy, scale=scale).then_inc(prep_act, 1)

            with act.Fori(0, GROUPS) as g:
                for w in range(WP):
                    act.wait_ge(xtr_done, g * XE + (2 * w + 1))
                    for j in range(3):
                        last = nc.scalar.copy(
                            xt_view[:, j, :, :, w],
                            ps[:, (2 * w) % 4, j * GP:(j + 1) * GP].rearrange("p (h b) -> p h b", h=HP))
                    last.then_inc(xt_act, 1)
                for k in range(GT):
                    act.wait_ge(emb_done, g * GT + (k + 1))
                    if k >= 2:
                        act.wait_ge(htr_done, g * GT + (k - 1))
                        act.wait_ge(hall_ready, g * GT + (k - 1))
                    nc.scalar.copy(hstage[k % 2][:], ps[0:T, 4 + k % 2, 0:E]).then_inc(hstage_ready, 1)
                act.wait_ge(htr_done, g * GT + GT)
                act.wait_ge(hall_ready, g * GT + GT)

            def exponent(L, t):
                at(act, L.sub_ready, t + 1)
                nc.scalar.activation(L.p[:, :, 0:S], L.p[:, :, 0:S], ACT.Exp).then_inc(L.exp_ready, 1)

            def take_q(t):
                at(act, L1.qk_done, t + 1)
                at(act, L1.scores_done, t)
                for c in range(2):
                    last = nc.scalar.activation(L1.qt[:, c, :], ps[0:C, L1.bq, c * T:(c + 1) * T],
                                                ACT.Identity, scale=SCALE, bias=qbias[:, c:c + 1])
                last.then_inc(L1.q_ready, 1)

            def take_qk(t):
                at(act, L2.qk_done, t + 1)
                at(act, L2.scores_done, t)
                at(act, L2.kbd_ready, t)
                nc.scalar.copy(L2.qk[:].rearrange("p c t -> p (c t)"),
                               ps[0:C, L2.bq, 0:4 * T]).then_inc(L2.k_ready, 1)

            def take_v(L, t):
                at(act, L.v_done, t + 1)
                at(act, L.pv_done, t)
                src = ps[:, L.bm, 0:E].rearrange("p (g e d) -> p g e d", g=PAIRS, e=2)
                for s in range(SEQ):
                    dst = L.vbd[:, s, :].rearrange("p (g e d) -> p g e d", g=PAIRS, e=2)
                    for e in range(2):
                        last = nc.scalar.copy(dst[e * PB:e * PB + S, :, e, :], src[s * PB:s * PB + S, :, e, :])
                last.then_inc(L.v_ready, 1)

            def take_pt(L, t):
                at(act, L.ptr_done, t + 1)
                for k, ready in ((0, L.pt_ready_a), (1, L.pt_ready_b)):
                    nc.scalar.copy(L.pt[:, 3 * k:3 * k + 3, :].rearrange("p g i -> p (g i)"),
                                   ps[0:PP, L.bs + k, 0:3 * PP]).then_inc(ready, 1)

            def take_y(L, t):
                at(act, L.pv_done, t + 1)
                at(act, L.proj_done, t)
                if L is L1:
                    for c in range(2):
                        last = nc.scalar.activation(L.yt[0:C, c, :], ps[0:C, L.bs, c * T:(c + 1) * T],
                                                    ACT.Identity, bias=b6[:, 4 + c:5 + c])
                else:
                    last = nc.scalar.copy(L.yt[0:C].rearrange("p c t -> p (c t)"), ps[0:C, L.bs, 0:2 * T])
                last.then_inc(L.yt_ready, 1)

            def take_h1(t):
                at(act, tr2_done, t + 1)
                at(act, L2.v_done, t)
                nc.scalar.copy(L2.ht[0:C].rearrange("p c (s q) -> p c s q", s=2)[:, :, :, 0:S],
                               ps[0:C, L1.bm, 0:2 * T].rearrange("p (c s j) -> p c s j", c=2, s=SEQ)
                               ).then_inc(L2.ht_ready, 1)

            def router_exp(t):
                at(act, nmax_ready, t + 1)
                nc.scalar.activation(ex[:], ps[0:PP, L2.bm, ER:ER + NE], ACT.Exp, bias=nmax[:, 0:1],
                                     accum_out=esum[:, 0:1]).then_inc(ex_ready, 1)

            def take_hw(t):
                at(act, hwtr_done, t + 1)
                nc.scalar.copy(L2.ht[C:C + 1 + NE, 0, 0:PP], ps[0:1 + NE, L2.bm, 128:128 + PP])
                nc.scalar.copy(hwt[:, 0:PP], ps[0:ER, L2.bm, 0:PP]).then_inc(hwt_ready, 1)

            def inverse_deviation(L, t):
                at(act, L.mv_ready, t + 1)
                at(act, L.ln_ready, t)
                nc.scalar.activation(L.lnv[:], L.mv[:, 1:2], ACT.Ln, bias=eps_col[:, 0:1]).then_inc(L.lnv_ready, 1)
                at(act, L.lnv_ready, t + 1)
                nc.scalar.activation(L.rstd[:], L.lnv[:], ACT.Exp, scale=-0.5).then_inc(L.rstd_ready, 1)

            act.wait_ge(prep_extra, 1)

            def iteration(i, live):
                a, b, c, d, e = i, i - 1, i - 2, i - 3, i - 4
                if live(2):
                    take_h1(c)
                if live(4):
                    take_y(L2, e)
                if live(3):
                    take_v(L2, d)
                if live(1):
                    exponent(L1, b)
                if live(2):
                    router_exp(c)
                if live(0):
                    take_q(a)
                if live(4):
                    inverse_deviation(L2, e)
                if live(1):
                    take_pt(L1, b)
                    take_y(L1, b)
                if live(2):
                    take_hw(c)
                if live(0):
                    take_v(L1, a)
                if live(3):
                    exponent(L2, d)
                if live(1):
                    inverse_deviation(L1, b)
                if live(2):
                    take_qk(c)
                if live(3):
                    take_pt(L2, d)

            run(act, iteration)

        @block.vector
        def _(dve):
            dve.wait_ge(consts_ready, 1)
            for n, (parts, rows, cols, dst, scale) in enumerate(prep):
                if n % 2 == 1:
                    dve.wait_ge(prep_tr, n + 1)
                    src = ps[0:rows, n % 8, 0:cols]
                    if len(dst.shape) == 3:
                        src = src.rearrange("p (a b) -> p a b", a=dst.shape[1])
                    if scale == 1.0:
                        last = nc.vector.tensor_copy(dst, src)
                    else:
                        last = nc.vector.tensor_scalar(dst, src, scale, None, ALU.mult)
                    last.then_inc(prep_dve, 1)
            dve.wait_ge(prep_dve, N_PREP // 2)
            dve.wait_ge(prep_act, (N_PREP + 1) // 2)
            for c in range(2):
                nc.vector.tensor_scalar(relk[:, c, :], relt[:], b6[:, 2 + c:3 + c], None, ALU.add)
            nc.vector.memset(two_rows[:], LORA_SCALE).then_inc(dve_consts, 1)
            dve.wait_ge(dve_consts, 1)
            nc.vector.memset(two_rows[0:1], 1.0).then_inc(dve_consts, 1)
            dve.wait_ge(dve_consts, 2)
            nc.vector.tensor_scalar(w2[C:C + 1 + NE, 0, :], ext_raw[:], two_rows[:, 0:1], None, ALU.mult)
            nc.vector.tensor_scalar(qbias[:], b6[:, 0:2], SCALE, None, ALU.mult).then_inc(prep_extra, 1)
            dve.wait_ge(prep_extra, 1)
            for w in (w2[:, 0, 0:E], w2[0:C, 1, 0:E], b2[:, 0:E]):
                nc.vector.tensor_scalar(w, w, SCALE, None, ALU.mult).then_inc(prep_extra, 1)

            def regroup(u, loaded):
                dve.wait_ge(x_loaded[u], loaded)
                for ch in range(CH):
                    nc.vector.tensor_copy(
                        xr[:, ch * WP:(ch + 1) * WP, :].rearrange("p w (q v) -> p q w v", q=PATCH),
                        xb[u][:, ch, :].rearrange("p (q w v) -> p q w v", q=PATCH, w=WP)).then_inc(xr_ready, 1)

            with dve.Fori(0, GROUPS // 2) as gg:
                for u in range(2):
                    regroup(u, gg * (16 * HP) + 16 * HP)
                    for w in range(WP):
                        dve.wait_ge(xtr_done, gg * (2 * XE) + (u * XE + 2 * w + 2))
                        for j in range(3):
                            last = nc.vector.tensor_copy(
                                xt_view[:, 3 + j, :, :, w],
                                ps[:, (2 * w + 1) % 4, j * GP:(j + 1) * GP].rearrange("p (h b) -> p h b", h=HP))
                        last.then_inc(xt_dve, 1)
                    for k in range(GT):
                        dve.wait_ge(htr_done, gg * (2 * GT) + (u * GT + k + 1))
                        nc.vector.tensor_copy(
                            ht_all[:, bass.ds(gg * (2 * GT * 2 * T) + (u * GT + k) * 2 * T, 2 * T)],
                            ps[0:C, 6 + k % 2, 0:2 * T]).then_inc(htall_ready, 1)
                    dve.wait_ge(emb_done, gg * (2 * GT) + (u + 1) * GT)
            dve.wait_ge(hall_ready, TILES)

            def score_view(L):
                return ps[0:PP, L.bs:L.bs + 2, 0:HC * S].rearrange("p b (h j) -> p b h j", h=HC)

            def probs_view(L):
                return L.p[:, :, 0:S].rearrange("p (b h) j -> p b h j", b=2)

            def subtract_max(L, t):
                at(dve, L.scores_done, t + 1)
                nc.vector.tensor_reduce(L.mx[:].rearrange("p (b h) -> p b h", b=2), score_view(L), AX.X,
                                        ALU.max).then_inc(L.mx_ready, 1)
                at(dve, L.mx_ready, t + 1)
                at(dve, L.ptr_done, t)
                nc.vector.tensor_tensor(
                    probs_view(L), score_view(L),
                    L.mx[:].rearrange("p (b h) -> p b h", b=2)[:, :, :, None].to_broadcast([PP, 2, HC, S]),
                    ALU.subtract).then_inc(L.sub_ready, 1)

            def sum_probs(L, t):
                at(dve, L.exp_ready, t + 1)
                nc.vector.tensor_reduce(L.sum[:], L.p[:, :, 0:S], AX.X, ALU.add).then_inc(L.sum_ready, 1)

            def invert_sums(L, t):
                at(dve, L.sum_ready, t + 1)
                nc.vector.reciprocal(L.rsum[:], L.sum[:]).then_inc(L.rsum_ready, 1)

            def scale_probs(L, t):
                at(dve, L.rsum_ready, t + 1)
                nc.vector.tensor_tensor(L.p[:, :, 0:S], L.p[:, :, 0:S],
                                        L.rsum[:, :, None].to_broadcast([PP, H, S]),
                                        ALU.mult).then_inc(L.p_ready, 1)

            def take_k(t):
                at(dve, L1.q_ready, t + 1)
                at(dve, L1.kbd_ready, t)
                nc.vector.tensor_tensor(
                    L1.kt.rearrange("p c (s j) -> p c s j", s=SEQ),
                    ps[0:C, L1.bq, 2 * T:4 * T].rearrange("p (c s j) -> p c s j", c=2, s=SEQ),
                    relk[:, :, None, :].to_broadcast([C, 2, SEQ, S]), ALU.add).then_inc(L1.k_ready, 1)

            def ln_stats(L, t):
                at(dve, L.proj_done, t + 1)
                if L is L2:
                    at(dve, h1_kept, t + 1)
                nc.vector.tensor_tensor(L.res[:], ps[0:T, L.bs + 1, 0:E], h_all[:, bass.ds(t * E, E)],
                                        ALU.add).then_inc(L.res_ready, 1)
                at(dve, L.res_ready, t + 1)
                nc.vector.bn_stats(L.st[:], L.res[:]).then_inc(L.st_ready, 1)

            def ln_aggregate(L, t):
                at(dve, L.st_ready, t + 1)
                nc.vector.memset(L.pad[:], 0.0)
                nc.vector.bn_aggr(L.mv[:], L.st[:]).then_inc(L.mv_ready, 1)

            def ln_apply(L, t):
                at(dve, L.rstd_ready, t + 1)
                if L is L1:
                    at(dve, tr2_done, t)
                    at(dve, h1_kept, t)
                    nc.vector.tensor_scalar(h1s[:], L.res[:], L.mv[:, 0:1], L.rstd[:, 0:1], ALU.subtract,
                                            ALU.mult).then_inc(L.ln_ready, 1)
                else:
                    at(dve, out_stored, t * 16)
                    nc.vector.tensor_scalar(o_sb[:], L.res[:], L.mv[:, 0:1], L.rstd[:, 0:1], ALU.subtract,
                                            ALU.mult).then_inc(L.ln_ready, 1)

            def router_max(t):
                at(dve, lora_done, t + 1)
                nc.vector.tensor_reduce(nmax[:], ps[0:PP, L2.bm, ER:ER + NE], AX.X, ALU.max,
                                        negate=True).then_inc(nmax_ready, 1)

            RS = 4

            def combine(t):
                def step(ins, k):
                    ins.then_inc(router_step, 1)
                    at(dve, router_step, t * RS + k)

                at(dve, ex_ready, t + 1)
                nc.vector.reciprocal(resum[:], esum[:])
                step(nc.vector.max(top8[:], ex[:]), 1)
                nc.vector.tensor_scalar(en[:], ex[:], resum[:, 0:1], None, ALU.mult)
                step(nc.vector.max_index(idx8[:], top8[:], ex[:]), 2)
                nc.vector.scalar_tensor_tensor(out=pick0[:], in0=iota8[:], scalar=idx8[:, 0:1], in1=en[:],
                                               op0=ALU.is_equal, op1=ALU.mult)
                step(nc.vector.scalar_tensor_tensor(out=pick1[:], in0=iota8[:], scalar=idx8[:, 1:2], in1=en[:],
                                                    op0=ALU.is_equal, op1=ALU.mult), 3)
                step(nc.vector.tensor_tensor(comb[:, 1:1 + NE], pick0[:], pick1[:], ALU.add), 4)
                nc.vector.tensor_tensor(
                    hw[:].rearrange("p (e r) -> p e r", e=NE),
                    ps[0:PP, L2.bm, 0:ER].rearrange("p (e r) -> p e r", e=NE),
                    comb[:, 1:1 + NE][:, :, None].to_broadcast([PP, NE, R]), ALU.mult).then_inc(hw_ready, 1)

            def iteration(i, live):
                a, b, c, d, e = i, i - 1, i - 2, i - 3, i - 4
                if live(1):
                    subtract_max(L1, b)
                if live(4):
                    ln_stats(L2, e)
                if live(2):
                    router_max(c)
                if live(1):
                    sum_probs(L1, b)
                if live(4):
                    ln_aggregate(L2, e)
                if live(1):
                    invert_sums(L1, b)
                    scale_probs(L1, b)
                if live(0):
                    take_k(a)
                if live(4):
                    ln_apply(L2, e)
                if live(2):
                    combine(c)
                if live(3):
                    subtract_max(L2, d)
                if live(1):
                    ln_stats(L1, b)
                if live(3):
                    sum_probs(L2, d)
                if live(1):
                    ln_aggregate(L1, b)
                if live(3):
                    invert_sums(L2, d)
                    scale_probs(L2, d)
                if live(1):
                    ln_apply(L1, b)

            run(dve, iteration)


_INS = ['x', 'L0_tok_W', 'L0_attn_w_attn', 'L0_attn_b_attn', 'L0_attn_w_proj', 'L0_attn_b_proj', 'L0_attn_rel_emb',
        'L0_ffn_Wg', 'L0_ffn_bg', 'L0_ffn_Wqkv', 'L0_ffn_bqkv', 'L0_ffn_Wproj', 'L0_ffn_bproj', 'L0_ffn_A',
        'L0_ffn_ba', 'L0_ffn_Bm', 'L0_ffn_bb']
_OUT = ((64, 49, 192), 'float32')


def kernel(**inputs):
    import numpy as _np
    import concourse.bacc as _bacc
    from concourse import mybir as _mybir
    from concourse.bass_utils import run_bass_kernel_spmd as _run

    nc = _bacc.Bacc("TRN2", target_bir_lowering=False, num_devices=1)
    arrays, args = {}, []
    for name in _INS:
        a = _np.ascontiguousarray(inputs[name])
        arrays[f"in_{name}"] = a
        args.append(nc.dram_tensor(f"in_{name}", a.shape, _mybir.dt.from_np(a.dtype), kind="ExternalInput").ap())
    args.append(nc.dram_tensor("out_0", _OUT[0], _mybir.dt.from_np(_np.dtype(_OUT[1])), kind="ExternalOutput").ap())
    build(nc, *args)
    r = _run(nc, [arrays], core_ids=[0])
    return r.results[0]["out_0"]
```

```python
from contextlib import ExitStack

import concourse.bass as bass
from concourse import mybir

F32 = mybir.dt.float32
BF16 = mybir.dt.bfloat16
U32 = mybir.dt.uint32
ALU = mybir.AluOpType
ACT = mybir.ActivationFunctionType
AX = mybir.AxisListType


def build(nc, x, tok_w, w_attn, b_attn, w_proj, b_proj, rel_emb, wg, bg, wqkv, bqkv, wproj2, bproj2,
          lora_a, lora_ba, lora_b, lora_bb, out):
    NB, CH, HI, WI = x.shape
    E, PD = tok_w.shape
    PATCH = 16
    HP, WP = HI // PATCH, WI // PATCH
    S = HP * WP
    SEQ = 2
    T = SEQ * S
    TILES = NB // SEQ
    GB = 16
    GROUPS = NB // GB
    M = HP * GB
    GM = WP
    PRODUCTS = GROUPS * GM
    GP = HP * GB
    H = 12
    D = E // H
    C = E // 2
    F = 128
    H0 = F // D
    F1 = E - F
    HEADS = ((0, H0), (H0, H))
    ORDER = ((0, 0, F), (F, E, F), (2 * F, F, F1), (2 * F + F1, E + F, F1 + E))
    KX = PD // 128
    NE, R, _ = lora_a.shape
    ER = NE * R
    QKV = 3 * E
    PB = 64
    PP = PB + S
    PAIRS = H // 2
    SCALE = float(D) ** -0.5
    LORA_SCALE = 32 / R
    EPS = 1e-5
    NEG = -1e30
    assert PD == KX * 128 and S <= PB and D * 2 == 32 and ER == 128 and 2 * F1 == 128 and E == 2 * C

    with ExitStack() as ctx:
        def sb(name, shape, dt=F32):
            return ctx.enter_context(nc.sbuf_tensor(name, shape, dt))

        def sem(name):
            return ctx.enter_context(nc.semaphore(name))

        ps = ctx.enter_context(nc.psum_tensor("ps", [128, 8, 512], F32))

        ident = sb("ident", [128, 128])
        ident_bf = sb("ident_bf", [128, 128], BF16)
        causal = sb("causal", [128, H0 * S], BF16)
        headmask = sb("headmask", [F, H0])
        headmask1 = sb("headmask1", [2 * F1, H - H0])
        iota8i = sb("iota8i", [PP, NE], mybir.dt.int32)
        iota8 = sb("iota8", [PP, NE])
        eps_col = sb("eps_col", [T, 1])
        two_rows = sb("two_rows", [1 + NE, 1])

        tokw_raw = sb("tokw_raw", [C, 2, PD])
        raw = [sb(f"raw{n}", [128, 6 * E]) for n in range(2)]
        wqkv_raw = raw[0][0:C, 0:6 * E].rearrange("p (m k) -> p m k", m=6)
        wproj_raw = raw[1][0:C, 0:2 * E].rearrange("p (m k) -> p m k", m=2)
        bm_raw = raw[1][0:C, 2 * E:2 * E + 6 * ER].rearrange("p (m e r) -> p m e r", m=6, e=NE)
        a_raw = sb("a_raw", [ER, E])
        g_raw = sb("g_raw", [NE, E])
        b_raw = sb("b_raw", [6, 128])
        rel_raw = sb("rel_raw", [S, H0, D])
        ext_raw = sb("ext_raw", [1 + NE, QKV])
        tokw = sb("tokw", [128, KX, E])
        w1 = sb("w1", [C, 2, QKV])
        p1 = sb("p1", [C + 1, 2, E])
        b6 = sb("b6", [128, 6])
        qbias = sb("qbias", [128, 2])
        relt = sb("relt", [128, S])
        relk = sb("relk", [128, 2, S])
        w2 = sb("w2", [C + 1 + NE, 2, QKV])
        b2 = sb("b2", [ER, QKV])
        p2 = sb("p2", [C + 1, 2, E])
        lora = sb("lora", [C + 1, 2, ER + NE])

        xb = sb("xb", [GP, CH, PATCH * WI])
        xr = sb("xr", [GP, CH * WP, PATCH * PATCH])
        xt = [sb(f"xt{u}", [128, KX, GB * S]) for u in range(2)]
        HS = 4
        hstage = [sb(f"hstage{u}", [M, E]) for u in range(HS)]
        h_all = sb("h_all", [T, TILES * E])
        ht_all = sb("ht_all", [C, 2, NB * S])

        class Layer:

            def __init__(self, n, bank):
                self.parts = (0, 1) if n == 1 else (1, 0)
                self.bq, self.bm, self.bs = bank, bank + 1, bank + 2
                self.ht = sb(f"ht{n}", [C + 1 + NE, 2, 128])
                self.qk = sb(f"qk{n}", [F, 2, T])
                self.q1 = sb(f"q1_{n}", [2 * F1, 128])
                self.k1 = sb(f"k1_{n}", [2 * F1, S])
                self.kbd = raw[n - 1][:, 0:SEQ * H0 * S].rearrange("p (s h j) -> p s h j", s=SEQ, h=H0)
                self.kbd1 = raw[n - 1][:, SEQ * H0 * S:(SEQ * H0 + H - H0) * S].rearrange("p (h j) -> p h j", h=H - H0)
                self.vbd = sb(f"vbd{n}", [128, SEQ, E])
                self.mx = sb(f"mx{n}", [PP, H])
                self.p = sb(f"probs{n}", [PP, H, 64])
                self.sum = sb(f"sum{n}", [PP, H])
                self.rsum = sb(f"rsum{n}", [PP, H])
                self.pt = sb(f"pt{n}", [PP, PAIRS, PP])
                self.yt = sb(f"yt{n}", [C + 1, 2, T])
                self.res = sb(f"res{n}", [T, E])
                self.st = sb(f"st{n}", [T, 6])
                self.pad = sb(f"pad{n}", [1, 1])
                self.mv = sb(f"mv{n}", [T, 2])
                self.lnv = sb(f"lnv{n}", [T, 1])
                self.rstd = sb(f"rstd{n}", [T, 1])
                self.ht_ready = sem(f"ht_ready{n}")
                self.qk_done = sem(f"qk_done{n}")
                self.v_done = sem(f"v_done{n}")
                self.q_ready = sem(f"q_ready{n}")
                self.k_ready = sem(f"k_ready{n}")
                self.kbd_ready = sem(f"kbd_ready{n}")
                self.v_ready = sem(f"v_ready{n}")
                self.scores_done = [sem(f"scores_done{n}_{c}") for c in range(2)]
                self.mx_ready = [sem(f"mx_ready{n}_{c}") for c in range(2)]
                self.sub_ready = [sem(f"sub_ready{n}_{c}") for c in range(2)]
                self.exp_ready = [sem(f"exp_ready{n}_{c}") for c in range(2)]
                self.sum_ready = sem(f"sum_ready{n}")
                self.rsum_ready = sem(f"rsum_ready{n}")
                self.p_ready = [sem(f"p_ready{n}_{c}") for c in range(2)]
                self.ptr_done = [sem(f"ptr_done{n}_{c}") for c in range(2)]
                self.pt_ready = [sem(f"pt_ready{n}_{c}") for c in range(2)]
                self.pv_done = [sem(f"pv_done{n}_{c}") for c in range(2)]
                self.yt_ready = sem(f"yt_ready{n}")
                self.proj_done = sem(f"proj_done{n}")
                self.res_ready = sem(f"res_ready{n}")
                self.st_ready = sem(f"st_ready{n}")
                self.mv_ready = sem(f"mv_ready{n}")
                self.lnv_ready = sem(f"lnv_ready{n}")
                self.rstd_ready = sem(f"rstd_ready{n}")
                self.ln_ready = sem(f"ln_ready{n}")

        L1 = Layer(1, 0)
        L2 = Layer(2, 4)
        L2.q_ready = L2.k_ready
        h1s = sb("h1s", [T, E])
        o_sb = sb("o_sb", [T, E])
        hwt = sb("hwt", [ER, 128])
        nmax = sb("nmax", [PP, 1])
        ex = sb("ex", [PP, NE])
        esum = sb("esum", [PP, 1])
        resum = sb("resum", [PP, 1])
        top8 = sb("top8", [PP, 8])
        idx8 = sb("idx8", [PP, 8], U32)
        en = sb("en", [PP, NE])
        pick0 = sb("pick0", [PP, NE])
        pick1 = sb("pick1", [PP, NE])
        comb = sb("comb", [PP, 1 + NE])
        hw = sb("hw", [PP, ER])

        tokw_loaded = sem("tokw_loaded")
        weights_loaded = sem("weights_loaded")
        x_loaded = [sem(f"x_loaded{ch}") for ch in range(CH)]
        x_rest = sem("x_rest")
        ident_ready = sem("ident_ready")
        rel_zeroed = sem("rel_zeroed")
        pool_step = sem("pool_step")
        consts_ready = sem("consts_ready")
        dve_consts = sem("dve_consts")
        prep_tr = sem("prep_tr")
        prep_act = sem("prep_act")
        prep_dve = sem("prep_dve")
        prep_extra = sem("prep_extra")
        biases_ready = sem("biases_ready")
        vbias_done = sem("vbias_done")
        xr_ready = [sem(f"xr_ready{ch}") for ch in range(CH)]
        xtr_done = sem("xtr_done")
        xt_act = sem("xt_act")
        xt_dve = sem("xt_dve")
        emb_done = sem("emb_done")
        hstage_ready = sem("hstage_ready")
        htr_done = sem("htr_done")
        htall_ready = sem("htall_ready")
        hall_ready = [sem(f"hall_ready{u}") for u in range(HS)]
        tr2_done = sem("tr2_done")
        lora_done = sem("lora_done")
        nmax_ready = sem("nmax_ready")
        ex_ready = sem("ex_ready")
        router_step = sem("router_step")
        hw_ready = sem("hw_ready")
        hwtr_done = sem("hwtr_done")
        comb_ready = sem("comb_ready")
        hwt_ready = sem("hwt_ready")
        h1_kept = sem("h1_kept")
        out_stored = sem("out_stored")

        BLOCKS = []
        for here, there, count in ORDER:
            while count > 0:
                m, p = here // C, here % C
                n = min(count, C - p)
                BLOCKS.append((m, p, there, n))
                here, there, count = here + n, there + n, count - n
        W_DMAS = 3 * len(ORDER) + 2 * len(BLOCKS) + 17

        prep = []
        for half in range(2):
            for k in range(0, KX, 3):
                prep.append(([(tokw_raw[:, half, (k + j) * 128:(k + j + 1) * 128], j * C) for j in range(3)],
                             128, 3 * C, tokw[:, k:k + 3, half * C:(half + 1) * C], 1.0))
        TOK_PREP = len(prep)
        for kc in range(2):
            for m in range(0, 6, 3):
                prep.append(([(wqkv_raw[:, m + j, kc * C:(kc + 1) * C], j * C) for j in range(3)],
                             C, 3 * C, w2[0:C, kc, m * C:(m + 3) * C], 1.0))
        for m in range(0, 6, 3):
            prep.append(([(bm_raw[:, m + j, :, :].rearrange("p e r -> p (e r)"), j * C) for j in range(3)],
                         ER, 3 * C, b2[:, m * C:(m + 3) * C], LORA_SCALE))
        for kc in range(2):
            prep.append(([(wproj_raw[:, j, kc * C:(kc + 1) * C], j * C) for j in range(2)],
                         C, 2 * C, p2[0:C, kc, :], 1.0))
            prep.append(([(a_raw[:, kc * C:(kc + 1) * C], 0), (g_raw[:, kc * C:(kc + 1) * C], ER)],
                         C, ER + NE, lora[0:C, kc, :], 1.0))
        prep.append(([(b_raw[:, :], 0)], 128, 6, b6[:, :], 1.0))
        prep.append(([(rel_raw[:, :, :].rearrange("p h d -> p (h d)"), 0)], 128, S, relt[:, :], 1.0))
        N_PREP = len(prep)
        PC = (WP + 1) // 2
        XE = CH * PC
        assert XE % 4 == 0 and M == GP and GM * M == GB * S

        def columns(n):
            return range(2 * (n % PC), min(2 * (n % PC) + 2, WP))

        def prep_bank(n):
            return n + 4 if n < TOK_PREP else n % 4

        def fill(g, k):
            if g + 1 < GROUPS:
                return [("pixels", n) for n in range(4 * (k - 3), 4 * (k - 2)) if 0 <= n < XE]
            return [("weights", n) for n in range(TOK_PREP + 2 * k, TOK_PREP + 2 * k + 2)
                    if n < N_PREP]

        def pieces(k):
            found, token = [], k * M
            while token < (k + 1) * M:
                n = min(T - token % T, (k + 1) * M - token)
                found.append((token - k * M, n, token // T, token % T))
                token += n
            return found

        def kept(K):
            return 16 * sum(len(pieces(n % GM)) for n in range(K % HS, K + 1, HS))

        STAGES = 5

        def run(eng, iteration):
            for i in range(STAGES):
                iteration(i, lambda s, i=i: i >= s)
            with eng.Fori(STAGES, TILES) as i:
                iteration(i, lambda s: True)
            for i in range(TILES, TILES + STAGES - 1):
                iteration(i, lambda s, i=i: i - s < TILES)

        def at(eng, semaphore, n):
            if not (isinstance(n, int) and n <= 0):
                eng.wait_ge(semaphore, n)

        block = ctx.enter_context(nc.Block())

        @block.sync
        def _(sp):
            def load_x(g, ch):
                src = x[g * GB:(g + 1) * GB, ch].rearrange("b (h q) w -> h b (q w)", q=PATCH)
                for hp in range(HP):
                    sp.dma_start(xb[hp * GB:(hp + 1) * GB, ch], src[hp]).then_inc(x_loaded[ch], 16)

            def load_group(g):
                src = x[g * GB:(g + 1) * GB].rearrange("b c (h q) w -> h b c (q w)", q=PATCH)
                for hp in range(HP):
                    sp.dma_start(xb[hp * GB:(hp + 1) * GB], src[hp]).then_inc(x_rest, 16)

            load_x(0, 0)
            sp.dma_start(tokw_raw[:], tok_w.rearrange("(h p) k -> p h k", p=C)).then_inc(tokw_loaded, 16)
            for ch in range(1, CH):
                load_x(0, ch)

            weights = []

            def load_w(dst, src):
                weights.append((dst, src))

            for here, there, n in ORDER:
                load_w(w1[:, :, here:here + n], w_attn[:, there:there + n].rearrange("(k p) n -> p k n", p=C))
            load_w(p1[0:C], w_proj.rearrange("(k p) n -> p k n", p=C))
            load_w(p1[C:C + 1, 0, :], b_proj.unsqueeze(0))
            for row, col, first, n in ((0, 0, 0, F), (1, 0, E, F), (2, 0, F, F1), (2, F1, F, F1),
                                       (3, 0, E + F, F1), (3, F1, E + F, F1), (4, 0, 2 * E, C), (5, 0, 2 * E + C, C)):
                load_w(b_raw[row:row + 1, col:col + n], b_attn[first:first + n].unsqueeze(0))
            load_w(rel_raw[1:S], rel_emb[0:S - 1, None, :].to_broadcast([S - 1, H0, D]))
            for m, p, there, n in BLOCKS:
                load_w(wqkv_raw[p:p + n, m, :], wqkv[there:there + n])
            for here, there, n in ORDER:
                load_w(ext_raw[0:1, here:here + n], bqkv[there:there + n].unsqueeze(0))
                load_w(ext_raw[1:1 + NE, here:here + n], lora_bb[:, there:there + n])
            load_w(wproj_raw, wproj2.rearrange("(m p) k -> p m k", p=C))
            load_w(p2[C:C + 1, 0, :], bproj2.unsqueeze(0))
            load_w(a_raw[:], lora_a.rearrange("e r k -> (e r) k"))
            load_w(g_raw[:], wg)
            load_w(lora[C:C + 1, 0, 0:ER], lora_ba.rearrange("e r -> (e r)").unsqueeze(0))
            load_w(lora[C:C + 1, 0, ER:ER + NE], bg.unsqueeze(0))
            for m, p, there, n in BLOCKS:
                load_w(bm_raw[p:p + n, m], lora_b[:, there:there + n, :].rearrange("e p r -> p e r"))
            assert len(weights) == W_DMAS

            for ch in range(CH):
                sp.wait_ge(xr_ready[ch], 1)
                load_x(1, ch)
            sp.wait_ge(rel_zeroed, 2)
            for g in range(GROUPS):
                for k in range(GM):
                    K = g * GM + k
                    sp.wait_ge(hstage_ready, K + 1)
                    for row, n, tile, first in pieces(k):
                        t = g * (GB // SEQ) + tile
                        sp.dma_start(h_all[first:first + n, t * E:(t + 1) * E],
                                     hstage[K % HS][row:row + n]).then_inc(hall_ready[K % HS], 16)
                    if g + 2 < GROUPS and k == 3:
                        for ch in range(CH):
                            sp.wait_ge(xr_ready[ch], g + 2)
                        load_group(g + 2)
                    for dst, src in weights[3 * K:3 * K + 3]:
                        sp.dma_start(dst, src).then_inc(weights_loaded, 16)

            out_rows = out.rearrange("b n e -> (b n) e")
            with sp.Fori(0, TILES) as t:
                sp.wait_ge(L2.ln_ready, t + 1)
                sp.dma_start(out_rows[bass.ds(t * T, T)], o_sb[:]).then_inc(out_stored, 16)
            sp.wait_ge(out_stored, 16 * TILES)

        @block.gpsimd
        def _(pool):
            steps = [0]

            def step(ins):
                steps[0] += 1
                ins.then_inc(pool_step, 1)
                pool.wait_ge(pool_step, steps[0])

            step(nc.gpsimd.memset(ident[:], 0.0))
            step(nc.gpsimd.affine_select(out=ident[:], in_=ident[:], compare_op=ALU.not_equal, fill=1.0,
                                         base=0, pattern=[[-1, 128]], channel_multiplier=1))
            nc.gpsimd.tensor_copy(ident_bf[:], ident[:]).then_inc(ident_ready, 1)
            nc.gpsimd.memset(rel_raw[:], 0.0).then_inc(rel_zeroed, 1)
            nc.gpsimd.memset(b_raw[:], 0.0).then_inc(rel_zeroed, 1)
            step(nc.gpsimd.memset(causal[:], 0.0))
            cz = causal[:].rearrange("p (h j) -> p h j", h=H0)
            for p0 in (0, PB):
                step(nc.gpsimd.affine_select(out=cz[p0:p0 + 64], in_=cz[p0:p0 + 64], compare_op=ALU.is_ge, fill=NEG,
                                             base=0, pattern=[[0, H0], [-1, S]], channel_multiplier=1))
            step(nc.gpsimd.memset(headmask[:], 1.0))
            step(nc.gpsimd.affine_select(out=headmask[:], in_=headmask[:], compare_op=ALU.is_ge, fill=0.0,
                                         base=0, pattern=[[-D, H0]], channel_multiplier=1))
            step(nc.gpsimd.affine_select(out=headmask[:], in_=headmask[:], compare_op=ALU.is_ge, fill=0.0,
                                         base=D - 1, pattern=[[D, H0]], channel_multiplier=-1))
            step(nc.gpsimd.tensor_tensor(headmask1[:], headmask[:, 0:H - H0], headmask[:, H - H0:H0], ALU.add))
            step(nc.gpsimd.iota(iota8i[:], pattern=[[1, NE]], base=0, channel_multiplier=0))
            step(nc.gpsimd.tensor_copy(iota8[:], iota8i[:]))
            for L in (L1, L2):
                step(nc.gpsimd.memset(L.ht[:], 0.0))
                step(nc.gpsimd.memset(L.vbd[:], 0.0))
                step(nc.gpsimd.memset(L.q1[:], 0.0))
                step(nc.gpsimd.memset(L.p[:], 0.0))
                step(nc.gpsimd.memset(L.yt[C:C + 1], 1.0))
            step(nc.gpsimd.memset(eps_col[:], EPS))
            step(nc.gpsimd.memset(hwt[:], 0.0))
            step(nc.gpsimd.memset(L2.ht[C:C + 1 + NE], 1.0))
            nc.gpsimd.memset(comb[:], 1.0).then_inc(consts_ready, 1)

            def take_input(t):
                if not (isinstance(t, int) and t == 0):
                    pool.wait_ge(L1.v_done, t)
                nc.gpsimd.tensor_copy(
                    L1.ht[0:C].rearrange("p c (s q) -> p c s q", s=2)[:, :, :, 0:S],
                    ht_all[:, :, bass.ds(t * T, T)].rearrange("p c (s j) -> p c s j", s=SEQ),
                ).then_inc(L1.ht_ready, 1)

            def block_diagonal(L, t):
                pool.wait_ge(L.k_ready, t + 1)
                if not (isinstance(t, int) and t == 0):
                    pool.wait_ge(L.scores_done[1], t)
                nc.gpsimd.tensor_tensor(
                    L.kbd,
                    L.qk[:, 1, :].rearrange("p (s j) -> p s j", s=SEQ)[:, :, None, :].to_broadcast([F, SEQ, H0, S]),
                    headmask[:, None, :, None].to_broadcast([F, SEQ, H0, S]), ALU.mult)
                nc.gpsimd.tensor_tensor(
                    L.kbd1, L.k1[:, None, :].to_broadcast([2 * F1, H - H0, S]),
                    headmask1[:, :, None].to_broadcast([2 * F1, H - H0, S]), ALU.mult).then_inc(L.kbd_ready, 1)

            def keep_h1(t):
                pool.wait_ge(L1.ln_ready, t + 1)
                nc.gpsimd.tensor_copy(h_all[:, bass.ds(t * E, E)], h1s[:]).then_inc(h1_kept, 1)

            def iteration(i, live):
                if live(0):
                    take_input(i)
                if live(3):
                    block_diagonal(L2, i - 3)
                if live(0):
                    block_diagonal(L1, i)
                if live(1):
                    keep_h1(i - 1)

            pool.wait_ge(htall_ready, PRODUCTS)
            pool.wait_ge(prep_tr, N_PREP)
            run(pool, iteration)

        @block.tensor
        def _(pe):
            def transpose_weight(n):
                parts, rows, cols, dst, scale = prep[n]
                if n >= TOK_PREP + 4:
                    pe.wait_ge(prep_act if n % 2 == 0 else prep_dve, (n - 4) // 2 + 1)
                for src, col in parts:
                    k = src.shape[0]
                    last = nc.tensor.transpose(
                        ps[0:rows, prep_bank(n), col:col + (cols if len(parts) == 1 else k)], src, ident[0:k, 0:k])
                last.then_inc(prep_tr, 1)

            def transpose_pixels(g, n):
                ch = n // PC
                pe.wait_ge(xr_ready[ch], g + 1)
                at(pe, xt_act if n % 2 == 0 else xt_dve, (g * XE + n - 4) // 2 + 1)
                for i, w in enumerate(columns(n)):
                    for j in range(2):
                        last = nc.tensor.transpose(
                            ps[:, n % 4, (2 * i + j) * GP:(2 * i + j + 1) * GP],
                            xr[:, ch * WP + w, j * 128:(j + 1) * 128], ident[0:GP, 0:GP])
                last.then_inc(xtr_done, 1)

            def embed(g, k):
                K = g * GM + k
                if k == 0:
                    pe.wait_ge(xt_act, (g + 1) * XE // 2)
                    pe.wait_ge(xt_dve, (g + 1) * XE // 2)
                at(pe, hstage_ready, K - 1)
                for kx in range(KX):
                    last = nc.tensor.matmul(ps[0:M, 4 + K % 2, 0:E], xt[g % 2][:, kx, k * M:(k + 1) * M],
                                            tokw[:, kx, :], start=(kx == 0), stop=(kx == KX - 1))
                last.then_inc(emb_done, 1)

            def htranspose(K):
                pe.wait_ge(hstage_ready, K + 1)
                at(pe, htall_ready, K - 1)
                for c in range(2):
                    last = nc.tensor.transpose(ps[0:C, 6 + K % 2, c * M:(c + 1) * M],
                                               hstage[K % HS][:, c * C:(c + 1) * C], ident[0:M, 0:M])
                last.then_inc(htr_done, 1)

            def bias_of_values():
                pe.wait_ge(prep_act, (N_PREP + 1) // 2)
                pe.wait_ge(prep_dve, N_PREP // 2)
                for c in range(2):
                    last = nc.tensor.matmul(ps[C:C + 1, 3, 0:E], b6[0:C, 4 + c:5 + c], p1[0:C, c, :],
                                            start=(c == 0), stop=(c == 1))
                last.then_inc(vbias_done, 1)

            pe.wait_ge(ident_ready, 1)
            for n in range(PC):
                transpose_pixels(0, n)
            pe.wait_ge(tokw_loaded, 16)
            for n in range(TOK_PREP):
                transpose_weight(n)
            for n in range(PC, XE):
                transpose_pixels(0, n)
            pe.wait_ge(prep_act, TOK_PREP // 2)
            pe.wait_ge(prep_dve, TOK_PREP // 2)
            for g in range(GROUPS):
                for k in range(GM):
                    embed(g, k)
                    for kind, n in fill(g, k):
                        if kind == "pixels":
                            transpose_pixels(g + 1, n)
                        else:
                            if n == TOK_PREP:
                                pe.wait_ge(weights_loaded, 16 * W_DMAS)
                            transpose_weight(n)
                    if g == GROUPS - 1 and k == GM - 1:
                        bias_of_values()
                    if g > 0 or k > 0:
                        htranspose(g * GM + k - 1)
            htranspose(PRODUCTS - 1)
            pe.wait_ge(htall_ready, PRODUCTS)
            pe.wait_ge(consts_ready, 1)

            def scores(L, t, parts=(0, 1)):
                if parts[0] == L.parts[0]:
                    at(pe, L.q_ready, t + 1)
                    at(pe, L.kbd_ready, t + 1)
                    at(pe, L.res_ready, t)
                for c in parts:
                    cols = (HEADS[c][1] - HEADS[c][0]) * S
                    if L is L1:
                        nc.tensor.matmul(ps[:, L.bs + c, 0:cols], ident_bf[:], causal[:, 0:cols], start=True, stop=False)
                    if c == 0:
                        for s in range(SEQ):
                            last = nc.tensor.matmul(ps[s * PB:s * PB + S, L.bs, 0:cols], L.qk[:, 0, s * S:(s + 1) * S],
                                                    L.kbd[:, s].rearrange("p h j -> p (h j)"),
                                                    start=(L is L2), stop=True)
                    else:
                        last = nc.tensor.matmul(ps[0:PP, L.bs + 1, 0:cols], L.q1[:, 0:PP],
                                                L.kbd1.rearrange("p h j -> p (h j)"), start=(L is L2), stop=True)
                    last.then_inc(L.scores_done[c], 1)

            def project_qk(L, chunks, w_of, t):
                at(pe, L.q_ready, t)
                at(pe, L.k_ready, t)
                for m in range(3):
                    for n, (k, src) in enumerate(chunks):
                        last = nc.tensor.matmul(
                            ps[:, L.bq, m * T:(m + 1) * T], w_of(n)[0:k, m * 128:(m + 1) * 128], src,
                            start=(n == 0), stop=(n == len(chunks) - 1))
                last.then_inc(L.qk_done, 1)

            def project_qk2(t):
                at(pe, L2.k_ready, t)

                def part(m, n, start, stop):
                    k, src = chunks2[n]
                    return nc.tensor.matmul(ps[:, L2.bq, m * T:(m + 1) * T], w_of2(n)[0:k, m * 128:(m + 1) * 128],
                                            tokens_of(src), start=start, stop=stop)

                for m in range(3):
                    part(m, 1, m == 0, False)
                at(pe, comb_ready, t + 1)
                for m in range(3):
                    part(m, 0, False, False)
                at(pe, hwt_ready, t + 1)
                for m in range(3):
                    last = part(m, 2, False, m == 2)
                last.then_inc(L2.qk_done, 1)

            def project_v(L, chunks, w_of, t):
                at(pe, L.v_ready, t)
                for n, (k, src) in enumerate(chunks):
                    last = nc.tensor.matmul(ps[0:PP, L.bm, 0:E], src[:, 0:PP], w_of(n)[0:k, 2 * E:3 * E],
                                            start=(n == 0), stop=(n == len(chunks) - 1))
                last.then_inc(L.v_done, 1)

            def transpose_probs(L, t):
                pf = L.p[:].rearrange("p h j -> p (h j)")
                for c in range(2):
                    at(pe, L.p_ready[c], t + 1)
                    for g in range(3):
                        k = (3 * c + g) * 128
                        last = nc.tensor.transpose(ps[0:PP, L.bs + c, g * PP:(g + 1) * PP], pf[:, k:k + PP],
                                                   ident[0:PP, 0:PP])
                    last.then_inc(L.ptr_done[c], 1)

            def weigh_values(L, t):
                at(pe, L.v_ready, t + 1)
                for c in range(2):
                    at(pe, L.pt_ready[c], t + 1)
                    for g in range(3):
                        for s in range(SEQ):
                            last = nc.tensor.matmul(
                                ps[32 * g:32 * g + 32, L.bs + c, s * S:(s + 1) * S],
                                L.vbd[0:PP, s, 32 * (3 * c + g):32 * (3 * c + g) + 32],
                                L.pt[:, 3 * c + g, s * PB:s * PB + S], start=True, stop=True)
                    last.then_inc(L.pv_done[c], 1)

            def out_project(L, w, t):
                at(pe, L.yt_ready, t + 1)
                for c, k in ((0, C + 1), (1, C)):
                    last = nc.tensor.matmul(ps[0:T, L.bs, 0:E], L.yt[0:k, c, :], w[0:k, c, :],
                                            start=(c == 0), stop=(c == 1))
                last.then_inc(L.proj_done, 1)

            def transpose_h1(t):
                at(pe, L1.ln_ready, t + 1)
                if not (isinstance(t, int) and t + 2 > TILES):
                    at(pe, L1.v_ready, t + 2)
                for c in range(2):
                    last = nc.tensor.transpose(ps[0:C, L1.bm, c * T:(c + 1) * T], h1s[:, c * C:(c + 1) * C],
                                               ident[0:T, 0:T])
                last.then_inc(tr2_done, 1)

            def route(t):
                at(pe, L2.ht_ready, t + 1)
                at(pe, L2.v_ready, t)
                for c, k in ((0, C + 1), (1, C)):
                    last = nc.tensor.matmul(ps[0:PP, L2.bm, 0:ER + NE], L2.ht[0:k, c, 0:PP],
                                            lora[0:k, c, :], start=(c == 0), stop=(c == 1))
                last.then_inc(lora_done, 1)

            def transpose_hw(t):
                at(pe, hw_ready, t + 1)
                nc.tensor.transpose(ps[0:1 + NE, L2.bm, 128:128 + PP], comb[:], ident[0:PP, 0:PP])
                nc.tensor.transpose(ps[0:ER, L2.bm, 0:PP], hw[:], ident[0:PP, 0:PP]).then_inc(hwtr_done, 1)

            def tokens_of(buffer):
                return buffer.rearrange("p (s q) -> p s q", s=2)[:, :, 0:S]

            chunks1 = [(C, L1.ht[0:C, 0, :]), (C, L1.ht[0:C, 1, :])]
            chunks2 = [(C + 1 + NE, L2.ht[:, 0, :]), (C, L2.ht[0:C, 1, :]), (ER, hwt[:, :])]
            w_of1 = lambda n: w1[:, n, :]
            w_of2 = lambda n: b2[:, :] if n == 2 else w2[:, n, :]

            for c in range(2):
                last = nc.tensor.matmul(ps[:, L2.bs + c, 0:H0 * S], ident_bf[:], causal[:], start=True, stop=True)

            def iteration(i, live):
                a, b, c, d, e = i, i - 1, i - 2, i - 3, i - 4
                if isinstance(i, int) and i == 1:
                    pe.wait_ge(prep_extra, 8)
                if live(1):
                    scores(L1, b)
                if live(4):
                    transpose_probs(L2, e)
                if live(2):
                    transpose_h1(c)
                if live(0):
                    project_qk(L1, [(C, ht_all[:, n, bass.ds(a * T, T)]) for n in range(2)], w_of1, a)
                if live(4):
                    weigh_values(L2, e)
                if live(0):
                    at(pe, L1.ht_ready, a + 1)
                    at(pe, L2.ht_ready, a - 1)
                    project_v(L1, chunks1, w_of1, a)
                if live(4):
                    out_project(L2, p2, e)
                if live(2):
                    route(c)
                if live(1):
                    transpose_probs(L1, b)
                if live(3):
                    scores(L2, d, (1,))
                if live(1):
                    weigh_values(L1, b)
                if live(3):
                    scores(L2, d, (0,))
                if live(1):
                    out_project(L1, p1, b)
                if live(2):
                    transpose_hw(c)
                    project_qk2(c)
                    project_v(L2, chunks2, w_of2, c)

            run(pe, iteration)

        xt_view = [xt[u][:].rearrange("p k (b h w) -> p k h b w", b=GB, h=HP) for u in range(2)]

        def pixel_copies(g, n):
            return [(xt_view[g % 2][:, 2 * (n // PC):2 * (n // PC) + 2, :, :, w],
                     ps[:, n % 4, 2 * i * GP:(2 * i + 2) * GP].rearrange("p (k h b) -> p k h b", k=2, h=HP))
                    for i, w in enumerate(columns(n))]

        def regroup_copy(ch):
            return (xr[:, ch * WP:(ch + 1) * WP, :].rearrange("p w (q v) -> p q w v", q=PATCH),
                    xb[:, ch, :].rearrange("p (q w v) -> p q w v", q=PATCH, w=WP))

        @block.scalar
        def _(act):
            nc.scalar.preload_act_table_set("natural_log_exp_and_others")

            def copy_weight(n):
                parts, rows, cols, dst, scale = prep[n]
                act.wait_ge(prep_tr, n + 1)
                src = ps[0:rows, prep_bank(n), 0:cols]
                if len(dst.shape) == 3:
                    src = src.rearrange("p (a b) -> p a b", a=dst.shape[1])
                nc.scalar.activation(dst, src, ACT.Copy, scale=scale).then_inc(prep_act, 1)

            def regroup(g, ch):
                if g < 2:
                    act.wait_ge(x_loaded[ch], 16 * HP * (g + 1))
                else:
                    act.wait_ge(x_rest, 16 * HP * (g - 1))
                at(act, xtr_done, (g - 1) * XE + (ch + 1) * PC)
                dst, src = regroup_copy(ch)
                nc.scalar.copy(dst, src).then_inc(xr_ready[ch], 1)

            def take_pixels(g, n):
                act.wait_ge(xtr_done, g * XE + n + 1)
                for dst, src in pixel_copies(g, n):
                    last = nc.scalar.copy(dst, src)
                last.then_inc(xt_act, 1)

            for n in range(0, PC, 2):
                take_pixels(0, n)
            for n in range(0, TOK_PREP, 2):
                copy_weight(n)
            regroup(0, 1)
            for n in range(PC, XE, 2):
                take_pixels(0, n)
            for g in range(GROUPS):
                for k in range(GM):
                    K = g * GM + k
                    act.wait_ge(emb_done, K + 1)
                    if K >= HS:
                        act.wait_ge(htr_done, K - HS + 1)
                        act.wait_ge(hall_ready[K % HS], kept(K - HS))
                    nc.scalar.copy(hstage[K % HS][:], ps[0:M, 4 + K % 2, 0:E]).then_inc(hstage_ready, 1)
                    if k == 1 and g + 1 < GROUPS:
                        regroup(g + 1, 1)
                    for kind, n in fill(g, k):
                        if n % 2 == 0:
                            if kind == "pixels":
                                take_pixels(g + 1, n)
                            else:
                                copy_weight(n)
            act.wait_ge(consts_ready, 1)

            def exponent(L, t, c):
                at(act, L.sub_ready[c], t + 1)
                p = L.p[:, HEADS[c][0]:HEADS[c][1], 0:S]
                nc.scalar.activation(p, p, ACT.Exp).then_inc(L.exp_ready[c], 1)

            def take_q(t):
                at(act, L1.qk_done, t + 1)
                at(act, L1.scores_done[1], t)
                nc.scalar.activation(L1.qk[:, 0, :], ps[:, L1.bq, 0:T], ACT.Identity, scale=SCALE, bias=qbias[:, 0:1])
                for s in range(SEQ):
                    last = nc.scalar.activation(L1.q1[s * F1:(s + 1) * F1, s * PB:s * PB + S],
                                                ps[0:F1, L1.bq, 2 * T + s * S:2 * T + (s + 1) * S],
                                                ACT.Identity, scale=SCALE, bias=qbias[0:F1, 1:2])
                last.then_inc(L1.q_ready, 1)

            def take_qk(t):
                at(act, L2.qk_done, t + 1)
                at(act, L2.scores_done[1], t)
                at(act, L2.kbd_ready, t)
                nc.scalar.copy(L2.qk[:].rearrange("p c t -> p (c t)"), ps[:, L2.bq, 0:2 * T])
                for s in range(SEQ):
                    cols = slice(2 * T + s * S, 2 * T + (s + 1) * S)
                    nc.scalar.copy(L2.q1[s * F1:(s + 1) * F1, s * PB:s * PB + S], ps[0:F1, L2.bq, cols])
                    last = nc.scalar.copy(L2.k1[s * F1:(s + 1) * F1, :], ps[F1:2 * F1, L2.bq, cols])
                last.then_inc(L2.k_ready, 1)

            def take_v(L, t):
                at(act, L.v_done, t + 1)
                at(act, L.pv_done[1], t)
                src = ps[:, L.bm, 0:E].rearrange("p (g e d) -> p g e d", g=PAIRS, e=2)
                for s in range(SEQ):
                    dst = L.vbd[:, s, :].rearrange("p (g e d) -> p g e d", g=PAIRS, e=2)
                    for e in range(2):
                        last = nc.scalar.copy(dst[e * PB:e * PB + S, :, e, :], src[s * PB:s * PB + S, :, e, :])
                last.then_inc(L.v_ready, 1)

            def take_pt(L, t, halves=(0, 1)):
                for c in halves:
                    at(act, L.ptr_done[c], t + 1)
                    nc.scalar.copy(L.pt[:, 3 * c:3 * c + 3, :].rearrange("p g i -> p (g i)"),
                                   ps[0:PP, L.bs + c, 0:3 * PP]).then_inc(L.pt_ready[c], 1)

            def take_y(L, t):
                at(act, L.proj_done, t)
                for c in range(2):
                    at(act, L.pv_done[c], t + 1)
                    last = nc.scalar.copy(L.yt[0:C, c, :], ps[0:C, L.bs + c, 0:T])
                last.then_inc(L.yt_ready, 1)

            def take_h1(t):
                at(act, tr2_done, t + 1)
                at(act, L2.v_done, t)
                nc.scalar.copy(L2.ht[0:C].rearrange("p c (s q) -> p c s q", s=2)[:, :, :, 0:S],
                               ps[0:C, L1.bm, 0:2 * T].rearrange("p (c s j) -> p c s j", c=2, s=SEQ)
                               ).then_inc(L2.ht_ready, 1)

            def router_exp(t):
                at(act, nmax_ready, t + 1)
                nc.scalar.activation(ex[:], ps[0:PP, L2.bm, ER:ER + NE], ACT.Exp, bias=nmax[:, 0:1],
                                     accum_out=esum[:, 0:1]).then_inc(ex_ready, 1)

            def take_hw(t):
                at(act, hwtr_done, t + 1)
                nc.scalar.copy(L2.ht[C:C + 1 + NE, 0, 0:PP], ps[0:1 + NE, L2.bm, 128:128 + PP]
                               ).then_inc(comb_ready, 1)
                nc.scalar.copy(hwt[:, 0:PP], ps[0:ER, L2.bm, 0:PP]).then_inc(hwt_ready, 1)

            def inverse_deviation(L, t):
                at(act, L.mv_ready, t + 1)
                at(act, L.ln_ready, t)
                nc.scalar.activation(L.lnv[:], L.mv[:, 1:2], ACT.Ln, bias=eps_col[:, 0:1]).then_inc(L.lnv_ready, 1)
                at(act, L.lnv_ready, t + 1)
                nc.scalar.activation(L.rstd[:], L.lnv[:], ACT.Exp, scale=-0.5).then_inc(L.rstd_ready, 1)

            act.wait_ge(biases_ready, 1)

            def iteration(i, live):
                a, b, c, d, e = i, i - 1, i - 2, i - 3, i - 4
                if live(4):
                    take_pt(L2, e, (0,))
                if live(2):
                    take_h1(c)
                if live(4):
                    take_pt(L2, e, (1,))
                if live(1):
                    exponent(L1, b, 0)
                    exponent(L1, b, 1)
                if live(4):
                    take_y(L2, e)
                if live(3):
                    take_v(L2, d)
                if live(0):
                    take_q(a)
                if live(1):
                    take_pt(L1, b)
                if live(2):
                    router_exp(c)
                if live(1):
                    take_y(L1, b)
                if live(4):
                    inverse_deviation(L2, e)
                if live(2):
                    take_hw(c)
                if live(0):
                    take_v(L1, a)
                if live(3):
                    exponent(L2, d, 1)
                    exponent(L2, d, 0)
                if live(1):
                    inverse_deviation(L1, b)
                if live(2):
                    take_qk(c)

            run(act, iteration)

        @block.vector
        def _(dve):
            def copy_weight(n):
                parts, rows, cols, dst, scale = prep[n]
                dve.wait_ge(prep_tr, n + 1)
                src = ps[0:rows, prep_bank(n), 0:cols]
                if len(dst.shape) == 3:
                    src = src.rearrange("p (a b) -> p a b", a=dst.shape[1])
                if scale == 1.0:
                    last = nc.vector.tensor_copy(dst, src)
                else:
                    last = nc.vector.tensor_scalar(dst, src, scale, None, ALU.mult)
                last.then_inc(prep_dve, 1)

            def regroup(g, ch):
                if g < 2:
                    dve.wait_ge(x_loaded[ch], 16 * HP * (g + 1))
                else:
                    dve.wait_ge(x_rest, 16 * HP * (g - 1))
                at(dve, xtr_done, (g - 1) * XE + (ch + 1) * PC)
                dst, src = regroup_copy(ch)
                nc.vector.tensor_copy(dst, src).then_inc(xr_ready[ch], 1)

            def take_pixels(g, n):
                dve.wait_ge(xtr_done, g * XE + n + 1)
                for dst, src in pixel_copies(g, n):
                    last = nc.vector.tensor_copy(dst, src)
                last.then_inc(xt_dve, 1)

            def take_ht(K):
                dve.wait_ge(htr_done, K + 1)
                nc.vector.tensor_copy(ht_all[:, :, K * M:(K + 1) * M],
                                      ps[0:C, 6 + K % 2, 0:2 * M].rearrange("p (c t) -> p c t", c=2)
                                      ).then_inc(htall_ready, 1)

            def finish_biases():
                dve.wait_ge(consts_ready, 1)
                dve.wait_ge(prep_dve, N_PREP // 2)
                dve.wait_ge(prep_act, (N_PREP + 1) // 2)
                for c in range(2):
                    nc.vector.tensor_scalar(relk[:, c, :], relt[:], b6[:, 2 * c + 1:2 * c + 2], None, ALU.add)
                nc.vector.tensor_scalar(qbias[:], b6[:].rearrange("p (c two) -> p c two", two=2)[:, 0:2, 0], SCALE, None,
                                        ALU.mult).then_inc(biases_ready, 1)

            def finish_weights():
                dve.wait_ge(vbias_done, 1)
                nc.vector.tensor_tensor(p1[C:C + 1, 0, :], ps[C:C + 1, 3, 0:E], p1[C:C + 1, 0, :],
                                        ALU.add).then_inc(prep_extra, 1)
                nc.vector.memset(two_rows[:], LORA_SCALE).then_inc(dve_consts, 1)
                dve.wait_ge(dve_consts, 1)
                nc.vector.memset(two_rows[0:1], 1.0).then_inc(dve_consts, 1)
                dve.wait_ge(dve_consts, 2)
                nc.vector.tensor_scalar(w2[C:C + 1 + NE, 0, :], ext_raw[:], two_rows[:, 0:1], None,
                                        ALU.mult).then_inc(prep_extra, 1)
                dve.wait_ge(prep_extra, 2)
                for queries in (slice(0, F), slice(2 * F, 2 * F + F1)):
                    for w in (w2[:, 0, queries], w2[0:C, 1, queries], b2[:, queries]):
                        nc.vector.tensor_scalar(w, w, SCALE, None, ALU.mult).then_inc(prep_extra, 1)

            regroup(0, 0)
            for n in range(1, PC, 2):
                take_pixels(0, n)
            for n in range(1, TOK_PREP, 2):
                copy_weight(n)
            for n in range(PC + 1, 2 * PC, 2):
                take_pixels(0, n)
            regroup(0, 2)
            for n in range(2 * PC + 1, XE, 2):
                take_pixels(0, n)
            for g in range(GROUPS):
                for k in range(GM):
                    if g + 1 < GROUPS and k in (0, 2):
                        regroup(g + 1, k)
                    for kind, n in fill(g, k):
                        if n % 2 == 1:
                            if kind == "pixels":
                                take_pixels(g + 1, n)
                            else:
                                copy_weight(n)
                    if g > 0 or k > 0:
                        take_ht(g * GM + k - 1)
                    if g == GROUPS - 1 and k == GM - 1:
                        finish_biases()
            take_ht(PRODUCTS - 1)
            for K in range(PRODUCTS - HS, PRODUCTS):
                dve.wait_ge(hall_ready[K % HS], kept(K))

            def largest(L, t, c):
                at(dve, L.scores_done[c], t + 1)
                lo, hi = HEADS[c]
                nc.vector.tensor_reduce(L.mx[:, lo:hi],
                                        ps[0:PP, L.bs + c, 0:(hi - lo) * S].rearrange("p (h j) -> p h j", j=S), AX.X,
                                        ALU.max).then_inc(L.mx_ready[c], 1)

            def subtract(L, t, c):
                at(dve, L.mx_ready[c], t + 1)
                at(dve, L.ptr_done[1], t)
                lo, hi = HEADS[c]
                nc.vector.tensor_tensor(
                    L.p[:, lo:hi, 0:S],
                    ps[0:PP, L.bs + c, 0:(hi - lo) * S].rearrange("p (h j) -> p h j", j=S),
                    L.mx[:, lo:hi, None].to_broadcast([PP, hi - lo, S]),
                    ALU.subtract).then_inc(L.sub_ready[c], 1)

            def sum_probs(L, t, c):
                at(dve, L.exp_ready[c], t + 1)
                lo, hi = HEADS[c]
                nc.vector.tensor_reduce(L.sum[:, lo:hi], L.p[:, lo:hi, 0:S], AX.X,
                                        ALU.add).then_inc(L.sum_ready, 1)

            def invert_sums(L, t):
                dve.wait_ge(L.sum_ready, 2 * t + 2)
                nc.vector.reciprocal(L.rsum[:], L.sum[:]).then_inc(L.rsum_ready, 1)

            def scale_probs(L, t, c):
                at(dve, L.rsum_ready, t + 1)
                lo, hi = HEADS[c]
                p = L.p[:, lo:hi, 0:S]
                nc.vector.tensor_tensor(p, p, L.rsum[:, lo:hi, None].to_broadcast([PP, hi - lo, S]),
                                        ALU.mult).then_inc(L.p_ready[c], 1)

            def take_k(t):
                at(dve, L1.q_ready, t + 1)
                at(dve, L1.kbd_ready, t)
                nc.vector.tensor_tensor(
                    L1.qk[:, 1, :].rearrange("p (s j) -> p s j", s=SEQ),
                    ps[:, L1.bq, T:2 * T].rearrange("p (s j) -> p s j", s=SEQ),
                    relk[:, 0:1, :].to_broadcast([F, SEQ, S]), ALU.add)
                for s in range(SEQ):
                    last = nc.vector.tensor_tensor(L1.k1[s * F1:(s + 1) * F1, :],
                                                   ps[F1:2 * F1, L1.bq, 2 * T + s * S:2 * T + (s + 1) * S],
                                                   relk[F1:2 * F1, 1, :], ALU.add)
                last.then_inc(L1.k_ready, 1)

            def add_residual(L, t):
                at(dve, L.proj_done, t + 1)
                if L is L2:
                    at(dve, h1_kept, t + 1)
                nc.vector.tensor_tensor(L.res[:], ps[0:T, L.bs, 0:E], h_all[:, bass.ds(t * E, E)],
                                        ALU.add).then_inc(L.res_ready, 1)

            def ln_stats(L, t):
                at(dve, L.res_ready, t + 1)
                nc.vector.bn_stats(L.st[:], L.res[:]).then_inc(L.st_ready, 1)

            def ln_aggregate(L, t):
                at(dve, L.st_ready, t + 1)
                nc.vector.memset(L.pad[:], 0.0)
                nc.vector.bn_aggr(L.mv[:], L.st[:]).then_inc(L.mv_ready, 1)

            def ln_apply(L, t):
                at(dve, L.rstd_ready, t + 1)
                if L is L1:
                    at(dve, tr2_done, t)
                    at(dve, h1_kept, t)
                    nc.vector.tensor_scalar(h1s[:], L.res[:], L.mv[:, 0:1], L.rstd[:, 0:1], ALU.subtract,
                                            ALU.mult).then_inc(L.ln_ready, 1)
                else:
                    at(dve, out_stored, t * 16)
                    nc.vector.tensor_scalar(o_sb[:], L.res[:], L.mv[:, 0:1], L.rstd[:, 0:1], ALU.subtract,
                                            ALU.mult).then_inc(L.ln_ready, 1)

            def router_max(t):
                at(dve, lora_done, t + 1)
                nc.vector.tensor_reduce(nmax[:], ps[0:PP, L2.bm, ER:ER + NE], AX.X, ALU.max,
                                        negate=True).then_inc(nmax_ready, 1)

            RS = 4

            def combine(t):
                def step(ins, k):
                    ins.then_inc(router_step, 1)
                    at(dve, router_step, t * RS + k)

                at(dve, ex_ready, t + 1)
                nc.vector.reciprocal(resum[:], esum[:])
                step(nc.vector.max(top8[:], ex[:]), 1)
                nc.vector.tensor_scalar(en[:], ex[:], resum[:, 0:1], None, ALU.mult)
                step(nc.vector.max_index(idx8[:], top8[:], ex[:]), 2)
                nc.vector.scalar_tensor_tensor(out=pick0[:], in0=iota8[:], scalar=idx8[:, 0:1], in1=en[:],
                                               op0=ALU.is_equal, op1=ALU.mult)
                step(nc.vector.scalar_tensor_tensor(out=pick1[:], in0=iota8[:], scalar=idx8[:, 1:2], in1=en[:],
                                                    op0=ALU.is_equal, op1=ALU.mult), 3)
                step(nc.vector.tensor_tensor(comb[:, 1:1 + NE], pick0[:], pick1[:], ALU.add), 4)
                nc.vector.tensor_tensor(
                    hw[:].rearrange("p (e r) -> p e r", e=NE),
                    ps[0:PP, L2.bm, 0:ER].rearrange("p (e r) -> p e r", e=NE),
                    comb[:, 1:1 + NE][:, :, None].to_broadcast([PP, NE, R]), ALU.mult).then_inc(hw_ready, 1)

            def iteration(i, live):
                a, b, c, d, e = i, i - 1, i - 2, i - 3, i - 4
                if live(1):
                    largest(L1, b, 0)
                    largest(L1, b, 1)
                    subtract(L1, b, 0)
                    subtract(L1, b, 1)
                    sum_probs(L1, b, 0)
                    sum_probs(L1, b, 1)
                    invert_sums(L1, b)
                    scale_probs(L1, b, 0)
                    scale_probs(L1, b, 1)
                if live(4):
                    add_residual(L2, e)
                if live(2):
                    router_max(c)
                if live(4):
                    ln_stats(L2, e)
                    ln_aggregate(L2, e)
                if live(0):
                    take_k(a)
                if isinstance(i, int) and i == 0:
                    finish_weights()
                if live(2):
                    combine(c)
                if live(3):
                    largest(L2, d, 1)
                    largest(L2, d, 0)
                    subtract(L2, d, 1)
                    subtract(L2, d, 0)
                if live(4):
                    ln_apply(L2, e)
                if live(1):
                    add_residual(L1, b)
                if live(3):
                    sum_probs(L2, d, 1)
                if live(1):
                    ln_stats(L1, b)
                if live(3):
                    sum_probs(L2, d, 0)
                if live(1):
                    ln_aggregate(L1, b)
                if live(3):
                    invert_sums(L2, d)
                    scale_probs(L2, d, 0)
                    scale_probs(L2, d, 1)
                if live(1):
                    ln_apply(L1, b)

            run(dve, iteration)


_INS = ['x', 'L0_tok_W', 'L0_attn_w_attn', 'L0_attn_b_attn', 'L0_attn_w_proj', 'L0_attn_b_proj', 'L0_attn_rel_emb',
        'L0_ffn_Wg', 'L0_ffn_bg', 'L0_ffn_Wqkv', 'L0_ffn_bqkv', 'L0_ffn_Wproj', 'L0_ffn_bproj', 'L0_ffn_A',
        'L0_ffn_ba', 'L0_ffn_Bm', 'L0_ffn_bb']
_OUT = ((64, 49, 192), 'float32')


def kernel(**inputs):
    import numpy as _np
    import concourse.bacc as _bacc
    from concourse import mybir as _mybir
    from concourse.bass_utils import run_bass_kernel_spmd as _run

    nc = _bacc.Bacc("TRN2", target_bir_lowering=False, num_devices=1)
    arrays, args = {}, []
    for name in _INS:
        a = _np.ascontiguousarray(inputs[name])
        arrays[f"in_{name}"] = a
        args.append(nc.dram_tensor(f"in_{name}", a.shape, _mybir.dt.from_np(a.dtype), kind="ExternalInput").ap())
    args.append(nc.dram_tensor("out_0", _OUT[0], _mybir.dt.from_np(_np.dtype(_OUT[1])), kind="ExternalOutput").ap())
    build(nc, *args)
    r = _run(nc, [arrays], core_ids=[0])
    return r.results[0]["out_0"]
```
